# Optimizing a Trainium2 kernel written in Bass

```python
import numpy as np
import jax
import jax.numpy as jnp

def _softmax(x, axis=-1):
    return jax.nn.softmax(x, axis=axis)

def _gelu(x):
    return jax.nn.gelu(x, approximate=True)

def _silu(x):
    return jax.nn.silu(x)

def _sigmoid(x):
    return jax.nn.sigmoid(x)

def _layernorm(x, axis=-1, eps=1e-05):
    m = jnp.mean(x, axis=axis, keepdims=True)
    v = jnp.var(x, axis=axis, keepdims=True)
    return (x - m) / jnp.sqrt(v + eps)

def _scatter_add(tgt, idx, src, axis=0):
    return tgt.at[idx].add(src)

def _segment_sum(src, seg, n):
    return jax.ops.segment_sum(src, seg, n)
kernel_name = 'mk_gnn_resnorm_d1_gnn_r16_9cac71'

def setup_inputs(seed: int=0):
    np.random.seed(seed)
    _w = jnp.asarray

    def _rec_inputs():
        import jax
        import jax.numpy as jnp
        _gk = jax.random.key(seed)
        x = -0.000202 + 1 * jax.random.normal(jax.random.fold_in(_gk, 1), (3125, 128), jnp.float32)
        src = jax.random.randint(jax.random.fold_in(_gk, 2), (100000,), 0, 3125, jnp.int32)
        dst = jnp.minimum((3125 * jax.random.uniform(jax.random.fold_in(_gk, 3), (100000,)) ** 2.0).astype(jnp.int32), 49999)
        _o = jnp.argsort(dst, stable=True)
        src = src[_o]
        dst = dst[_o]
        edge_attr_16 = -0.000107899 + 1.00008 * jax.random.normal(jax.random.fold_in(_gk, 12), (100000, 16), jnp.float32)
        return (x, src, dst, edge_attr_16)
    x, src, dst, edge_attr_16 = _rec_inputs()

    def _L0_gnn_setup():
        import jax, jax.numpy as jnp
        import numpy as np
        N, E, D, EF, L = (3125, 12500, 128, 16, 3)
        key = jax.random.key(seed)
        ks = jax.random.split(key, 8)
        nf = jax.random.normal(ks[0], (N, D), jnp.float32)
        ef = jax.random.normal(ks[1], (E, EF), jnp.float32)
        src = jax.random.randint(ks[2], (E,), 0, N, dtype=jnp.int32)
        dst = jax.random.randint(ks[3], (E,), 0, N, dtype=jnp.int32)
        We1 = jax.random.normal(ks[4], (L, 2 * D + EF, D), jnp.float32) / jnp.sqrt(2.0 * D + EF)
        We2 = jax.random.normal(ks[5], (L, D, D), jnp.float32) / jnp.sqrt(1.0 * D)
        Wn1 = jax.random.normal(ks[6], (L, 2 * D, D), jnp.float32) / jnp.sqrt(2.0 * D)
        Wn2 = jax.random.normal(ks[7], (L, D, D), jnp.float32) / jnp.sqrt(1.0 * D)
        return dict(nf=nf, ef=ef, src=src, dst=dst, We1=We1, We2=We2, Wn1=Wn1, Wn2=Wn2)
    _L0_gnn_all = _L0_gnn_setup()
    _L0_gnn_in = {k: v for k, v in _L0_gnn_all.items() if k in ('We1', 'We2', 'Wn1', 'Wn2')}
    del _L0_gnn_all
    return {'x': x, 'src': src, 'dst': dst, 'edge_attr_16': edge_attr_16, 'L0_gnn_We1': _L0_gnn_in['We1'], 'L0_gnn_We2': _L0_gnn_in['We2'], 'L0_gnn_Wn1': _L0_gnn_in['Wn1'], 'L0_gnn_Wn2': _L0_gnn_in['Wn2']}

def reference(x, src, dst, edge_attr_16, L0_gnn_We1, L0_gnn_We2, L0_gnn_Wn1, L0_gnn_Wn2):
    import jax
    import jax.numpy as jnp

    def _L0_gnn_ref(nf, ef, src, dst, We1, We2, Wn1, Wn2):
        import jax, jax.numpy as jnp
        import numpy as np
        N, E, D, EF, L = (3125, 12500, 128, 16, 3)
        s2 = jnp.concatenate([src, dst])
        d2 = jnp.concatenate([dst, src])
        ef2 = jnp.concatenate([ef, ef], axis=0)
        h_prev = nf
        for l in range(L):
            e_in = jnp.concatenate([h_prev[s2], h_prev[d2], ef2], axis=-1)
            msg = jax.nn.leaky_relu(e_in @ We1[l]) @ We2[l]
            red = jax.ops.segment_sum(msg, d2, num_segments=N)
            n_in = jnp.concatenate([h_prev, red], axis=-1)
            out = jax.nn.leaky_relu(n_in @ Wn1[l]) @ Wn2[l]
            h_prev = out + h_prev
        return out
    x = _layernorm(x + _L0_gnn_ref(x, edge_attr_16, src, dst, L0_gnn_We1, L0_gnn_We2, L0_gnn_Wn1, L0_gnn_Wn2), axis=-1)
    return x

_drawn_inputs = setup_inputs


def setup_inputs(seed=0):
    import zlib

    import numpy as np

    out = dict(_drawn_inputs(seed))
    spreads = {}
    factors = {'edge_attr_16': 6.146}
    for name, (base, spread) in spreads.items():
        noise = np.random.default_rng([zlib.crc32(name.encode()), seed]).standard_normal(out[name].shape)
        drawn = base * np.exp(spread * noise) if base else spread * noise
        out[name] = jnp.asarray(drawn.astype(out[name].dtype))
    for name, factor in factors.items():
        out[name] = (out[name] * factor).astype(out[name].dtype)
    return out
```

```python
from contextlib import ExitStack

import concourse.bass as bass
from concourse import mybir

P = 128
N, E, D, EF, L = 3125, 100000, 128, 16, 3
NB = -(-N // P)
NODES = NB * P
COLS = 784
PADS = P * COLS - E
BUCKETS = NB * (NB + 1) // 2 + 1
CHUNK = 8
ITER = 2 * CHUNK
TILES = 1120
LIVE_BOUND = (E + (BUCKETS - 1) * (P - 1)) // P + -(-PADS // P)
LAG = 3
assert LIVE_BOUND + 2 * LAG <= TILES and TILES % ITER == 0
CHUNKS = TILES // CHUNK
TURNS = TILES // ITER
PAIRS = ITER // 2
RING = 4
RW = EF + 2
GROUP = 14
GTURNS = COLS // (2 * GROUP)
MAPQ = -(-(TILES + 2 * LAG) // P)
TW = 3 * D
BANK = 512
BANKS = -(-NODES // BANK)
AHEAD = 1
SLOPE = 0.01
DEAD = 1000
EXP_MASK = 0x7F800000
EXP1 = 1 << 23

ALU = mybir.AluOpType
ACT = mybir.ActivationFunctionType
F32 = mybir.dt.float32
F16 = mybir.dt.float16
I32 = mybir.dt.int32
U32 = mybir.dt.uint32
AX_X = mybir.AxisListType.X
ds = bass.DynSlice


def build(nc, x, src, dst, ef, We1, We2, Wn1, Wn2, c_iota, c_part, c_tri, c_ident, c_tiles, c_steps, out):
    records = nc.dram_tensor("records", [TILES * P, RW], F32)
    feat_d = nc.dram_tensor("feat_d", [CHUNKS + 1, 4 * EF, CHUNK * P], F16)
    nums_d = nc.dram_tensor("nums_d", [CHUNKS + 1, 2 * CHUNK, P], F16)
    map_d = nc.dram_tensor("map_d", [MAPQ * P, 2], I32)

    with ExitStack() as ctx:
        def sb(name, shape, dt):
            return ctx.enter_context(nc.sbuf_tensor(name, shape, dt))

        def sem(name):
            return ctx.enter_context(nc.semaphore(name))

        sums = ctx.enter_context(nc.psum_tensor("sums", [P, BANKS * BANK], F32))
        gath = ctx.enter_context(nc.psum_tensor("gath", [P, BANK], F32))

        def bank(n):
            return sums[:, n * BANK:(n + 1) * BANK]

        iota = sb("iota", [P, 384], F16)
        part = sb("part", [P, 1], F32)
        tri = sb("tri", [P, 3, P], F16)
        ident = sb("ident", [P, P], F32)
        ident16 = sb("ident16", [P, P], F16)
        tiles_c = sb("tiles_c", [P, MAPQ], F32)
        steps_c = sb("steps_c", [P, 2, BUCKETS], F32)
        big = sb("big", [P, COLS * EF], F32)
        pre = sb("pre", [P, NB * TW], F32)
        src_t, dst_t, lo_n, hi_n, lo_b, hi_b = (pre[:, k * COLS:(k + 1) * COLS].bitcast(I32) for k in range(6))
        hot_words = 2 * GROUP * BUCKETS // 2
        onehot = pre[:, 6 * COLS:6 * COLS + hot_words].bitcast(F16).rearrange("p (g b) -> p g b", b=BUCKETS)
        numb = sb("numb", [P, 2, CHUNK * 2 * P], F16)
        gsel = sb("gsel", [P, 2, CHUNK * 2 * P], F16)
        fchunk = sb("fchunk", [4 * EF, 2, CHUNK * P], F16)
        loc = numb[:, :, :].rearrange("p h e -> p (h e)").bitcast(F32)[:, 0:2 * COLS]\
            .rearrange("p (j s) -> p j s", s=2)
        key = gsel[:, :, :].rearrange("p h e -> p (h e)").bitcast(F32)[:, 0:COLS]
        featT = fchunk
        keyc = sb("keyc", [P, 2 * GROUP], F32)
        scrap = sb("scrap", [P, BUCKETS], F32)
        cnt_i = sb("cnt_i", [P, BUCKETS], I32)
        cnt_f = sb("cnt_f", [P, BUCKETS], F32)
        tile_end = sb("tile_end", [P, BUCKETS], F32)
        tile_beg = sb("tile_beg", [P, BUCKETS], F16)
        zeros = sb("zeros", [P, BUCKETS], F32)
        zeros16 = sb("zeros16", [P, BUCKETS], F16)
        map_f = sb("map_f", [P, MAPQ, 2], F32)
        map_i = sb("map_i", [P, MAPQ, 2], I32)
        map_row = sb("map_row", [1, MAPQ * P * 2], I32)
        slot_f = sb("slot_f", [P, GROUP], F32)
        slot_i = sb("slot_i", [P, GROUP], I32)
        rowa = sb("rowa", [P, GROUP], I32)
        rowb = sb("rowb", [P, GROUP], I32)
        rowi = sb("rowi", [P, 2, GROUP], I32)
        rec = sb("rec", [P, 2, GROUP, RW], F32)
        blank = sb("blank", [P, CHUNK, RW], F32)
        recc = sb("recc", [P, 2, CHUNK, RW], F32)
        stack = sb("stack", [P, 2, CHUNK, 4, EF], F16)
        num16 = sb("num16", [P, 2, CHUNK * 2], F16)
        numT = sb("numT", [2 * CHUNK, 2, P], F16)
        numcol = sb("numcol", [P, TILES * 2], F32)
        xn = sb("xn", [P, NB, D], F32)
        hT = sb("hT", [P, NODES], F32)
        t_hi = pre[:, 0:NB * TW // 2].bitcast(F16)
        t_lo = pre[:, NB * TW // 2:NB * TW].bitcast(F16)
        t_hi3 = t_hi[:, :].rearrange("p (b w) -> p b w", w=TW)
        t_lo3 = t_lo[:, :].rearrange("p (b w) -> p b w", w=TW)
        ab = big[:, 0:NB * 2 * D]
        ab3 = ab.rearrange("p (b w) -> p b w", w=2 * D)
        sumS = big[:, 0:NODES]
        zbuf = big[:, NODES:2 * NODES]
        outT = big[:, 2 * NODES:3 * NODES]
        y = big[:, 0:NODES].rearrange("p (b f) -> p b f", f=D)
        msg = big[:, 3 * NODES:3 * NODES + RING * 4 * D].rearrange("p (r f) -> p r f", r=RING)
        wab = sb("wab", [P, 2, D], F32)
        wc = sb("wc", [4 * EF, D], F32)
        wcs = sb("wcs", [4 * EF, D], F32)
        wch = sb("wch", [4 * EF, D], F16)
        wst = sb("wst", [4 * EF, 2, D], F16)
        we2 = sb("we2", [P, D], F32)
        we2T = sb("we2T", [P, D], F32)
        wn1 = sb("wn1", [P, 2, D], F32)
        w21 = sb("w21", [P, D], F32)
        wn2 = sb("wn2", [P, D], F32)
        efmax = sb("efmax", [P, 2], F32)
        sc_ef = sb("sc_ef", [P, 2], F32)
        abmax = sb("abmax", [P, 16], F32)
        mx = sb("mx", [P, 2], F32)
        mxa = sb("mxa", [P, 2], F32)
        bnd = sb("bnd", [P, 2], F32)
        sc = sb("sc", [P, 2], F32)
        sc_w = sb("sc_w", [P, 1], F32)
        ebits = sb("ebits", [P, 2], I32)
        numc = sb("numc", [P, ITER * 2], F32)
        ssel = sb("ssel", [P, ITER, 2, P], F16)
        m_hi = sb("m_hi", [P, RING, 4 * D], F16)
        m_lo = sb("m_lo", [P, RING, 4 * D], F16)
        stats = sb("stats", [P, NB, 6], F32)
        mv = sb("mv", [P, NB, 2], F32)
        rstd = sb("rstd", [P, NB], F32)

        s_const = sem("s_const")
        s_edges = sem("s_edges")
        s_ef = sem("s_ef")
        s_x = sem("s_x")
        blank_set = sem("blank_set")
        blanked = sem("blanked")
        dve_seq = sem("dve_seq")
        id16_ready = sem("id16_ready")
        efmax_ready = sem("efmax_ready")
        efmax_all = sem("efmax_all")
        scef_ready = sem("scef_ready")
        hT_ps = sem("hT_ps")
        hT_in = sem("hT_in")
        keyc_set = sem("keyc_set")
        hot_set = sem("hot_set")
        hist_half = sem("hist_half")
        beg_ready = sem("beg_ready")
        map_ready = sem("map_ready")
        map_out = sem("map_out")
        map_in = sem("map_in")
        rank_set = sem("rank_set")
        rank_read = sem("rank_read")
        rows_seq = sem("rows_seq")
        rows_set = sem("rows_set")
        rec_set = sem("rec_set")
        moved = [sem(f"moved{h}") for h in range(2)]
        recc_in = [sem(f"recc_in{h}") for h in range(2)]
        recc_used = [sem(f"recc_used{h}") for h in range(2)]
        fhi_set = sem("fhi_set")
        flo_set = sem("flo_set")
        fst_set = sem("fst_set")
        tr_done = sem("tr_done")
        featT_set = sem("featT_set")
        numT_set = sem("numT_set")
        feat_out = [sem(f"feat_out{h}") for h in range(2)]
        nums_out = [sem(f"nums_out{h}") for h in range(2)]
        wrap_out = sem("wrap_out")
        w_in = sem("w_in")
        w2t_ps = sem("w2t_ps")
        w2t_set = sem("w2t_set")
        w21_ps = sem("w21_ps")
        w21_set = sem("w21_set")
        ab_ps = sem("ab_ps")
        ab_set = sem("ab_set")
        ab_maxed = sem("ab_maxed")
        mx_set = sem("mx_set")
        mx_all = sem("mx_all")
        sc_seq = sem("sc_seq")
        sc_set = sem("sc_set")
        thi_set = sem("thi_set")
        tables_set = sem("tables_set")
        wst_set = sem("wst_set")
        sums_zero = sem("sums_zero")
        numb_in = [sem(f"numb_in{h}") for h in range(2)]
        fchunk_in = [sem(f"fchunk_in{h}") for h in range(2)]
        gsel_set = sem("gsel_set")
        numc_set = sem("numc_set")
        gath_done = sem("gath_done")
        x_set = sem("x_set")
        msg_set = sem("msg_set")
        mhi_set = sem("mhi_set")
        mlo_set = sem("mlo_set")
        sum_done = sem("sum_done")
        sums_out = sem("sums_out")
        z_ps = sem("z_ps")
        z_set = sem("z_set")
        zl_set = sem("zl_set")
        o_ps = sem("o_ps")
        o_set = sem("o_set")
        h_set = sem("h_set")
        y_ps = sem("y_ps")
        y_seq = sem("y_seq")
        var_set = sem("var_set")
        std_set = sem("std_set")
        y_set = sem("y_set")
        s_out = sem("s_out")
        pool_go = sem("pool_go")
        pe_go = sem("pe_go")

        AB_STEPS = -(-NB // 2)
        T_PARTS = 5
        T_BLOCKS = NB // T_PARTS
        WIDE = [(n, min(BANK, NODES - n * BANK)) for n in range(BANKS)]
        YSTEPS = -(-NB // 4)
        W_DMAS = 8
        PADDED_MAP = 2 * LAG
        P0 = TURNS * PAIRS

        LOC_STEP = 12

        block = ctx.enter_context(nc.Block())

        @block.sync
        def _(sp):
            sp.dma_start(iota[:, :], c_iota).then_inc(s_const, 16)
            sp.dma_start(part[:, :], c_part).then_inc(s_const, 16)
            sp.dma_start(src_t[:, :], src.rearrange("(p j) -> p j", p=P)).then_inc(s_edges, 16)
            sp.dma_start(dst_t[:, :], dst.rearrange("(p j) -> p j", p=P)).then_inc(s_edges, 16)
            sp.dma_start(tri[:, :, :], c_tri).then_inc(s_const, 16)
            sp.dma_start(ident[:, :], c_ident).then_inc(s_const, 16)
            sp.dma_start(tiles_c[:, :], c_tiles).then_inc(s_const, 16)
            sp.dma_start(steps_c[:, :, :], c_steps).then_inc(s_const, 16)
            sp.dma_start(big[:, :], ef.rearrange("(p j) f -> p (j f)", p=P)).then_inc(s_ef, 16)
            sp.dma_start(xn[:, :, :], x.rearrange("(b p) f -> p b f", p=P)).then_inc(s_x, 16)
            sp.wait_ge(blank_set, 2)
            for c0, c1 in ((2, CHUNKS // 2), (CHUNKS // 2, CHUNKS)):
                sp.dma_start(records[c0 * CHUNK * P:c1 * CHUNK * P, :].rearrange("(c p t) f -> p c (t f)", p=P, t=CHUNK),
                             blank[:, :, :].rearrange("p t f -> p (t f)").unsqueeze(1)
                             .to_broadcast([P, c1 - c0, CHUNK * RW])).then_inc(blanked, 16)
            for h in range(2):
                sp.dma_start(feat_d[CHUNKS, h * P // 4:(h + 1) * P // 4, 0:RW], blank[0:P // 4, 0, :].bitcast(F16)[:, 0:RW])\
                  .then_inc(feat_out[h], 16)
                sp.dma_start(nums_d[CHUNKS, h * CHUNK:(h + 1) * CHUNK, 0:RW], blank[0:CHUNK, 0, :].bitcast(F16)[:, 0:RW])\
                  .then_inc(nums_out[h], 16)
            sp.wait_ge(map_ready, 1)
            sp.dma_start(map_d[:, :].rearrange("(q p) s -> p q s", p=P), map_i[:, :, :]).then_inc(map_out, 16)
            sp.wait_ge(map_out, 16)
            sp.dma_start(map_row[:, :], map_d[:, :].rearrange("(a q) s -> a (q s)", a=1)).then_inc(map_in, 16)
            with sp.Fori(0, CHUNKS // 2) as it:
                for h in range(2):
                    sp.wait_ge(featT_set, it * 2 + h + 1 + AHEAD)
                    sp.dma_start(feat_d[ds(it * 2 + h, 1), :, :].rearrange("a k e -> (a k) e"),
                                 featT[:, h, :]).then_inc(feat_out[h], 16)
                    sp.wait_ge(numT_set, it * 2 + h + 1 + AHEAD)
                    sp.dma_start(nums_d[ds(it * 2 + h, 1), :, :].rearrange("a k e -> (a k) e"),
                                 numT[:, h, :]).then_inc(nums_out[h], 16)
            for h in range(2):
                sp.wait_ge(feat_out[h], 16 * (CHUNKS // 2 + 1))
                sp.wait_ge(nums_out[h], 16 * (CHUNKS // 2 + 1))
            sp.dma_start(feat_d[CHUNKS, :, :], feat_d[0, :, :]).then_inc(wrap_out, 16)
            sp.dma_start(nums_d[CHUNKS, :, :], nums_d[0, :, :]).then_inc(wrap_out, 16)
            sp.wait_ge(wrap_out, 32)

            def load_chunk(c, h):
                sp.dma_start(numb[:, h, :], nums_d[ds(c, 1), :, :].rearrange("a k e -> a (k e)")
                             .to_broadcast([P, CHUNK * 2 * P])).then_inc(numb_in[h], 16)
                sp.dma_start(fchunk[:, h, :], feat_d[ds(c, 1), :, :].rearrange("a k e -> (a k) e"))\
                  .then_inc(fchunk_in[h], 16)

            load_chunk(0, 0)
            with sp.Fori(0, L) as l:
                sp.wait_ge(o_ps, l * BANKS + AHEAD)
                sp.dma_start(wab[:, :, :], We1[ds(l, 1), 0:2 * D, :].rearrange("a (s k) f -> k (a s) f", s=2))\
                  .then_inc(w_in, 16)
                for r in range(4):
                    sp.dma_start(wc[r * EF:(r + 1) * EF, :],
                                 We1[ds(l, 1), 2 * D:2 * D + EF, :].rearrange("a k f -> (a k) f")).then_inc(w_in, 16)
                sp.dma_start(we2[:, :], We2[ds(l, 1), :, :].rearrange("a k f -> (a k) f")).then_inc(w_in, 16)
                sp.dma_start(wn1[:, :, :], Wn1[ds(l, 1), :, :].rearrange("a (s k) f -> k (a s) f", s=2))\
                  .then_inc(w_in, 16)
                sp.dma_start(wn2[:, :], Wn2[ds(l, 1), :, :].rearrange("a k f -> (a k) f")).then_inc(w_in, 16)
                with sp.Fori(0, TURNS) as it:
                    for h in range(2):
                        chunk = it * 2 + h
                        sp.wait_ge(gsel_set, l * CHUNKS + chunk + 1)
                        sp.wait_ge(gath_done, l * P0 + chunk * (CHUNK // 2) + AHEAD)
                        load_chunk(chunk + 1, 1 - h)
            sp.wait_ge(y_set, 1)
            full = N // P
            sp.dma_start(out[0:full * P, :].rearrange("(b p) f -> p b f", p=P), y[:, 0:full, :]).then_inc(s_out, 16)
            sp.dma_start(out[full * P:N, :], y[0:N - full * P, full, :]).then_inc(s_out, 16)
            sp.wait_ge(s_out, 32)
            sp.wait_ge(numb_in[0], 16 * (1 + L * TURNS))
            sp.wait_ge(fchunk_in[0], 16 * (1 + L * TURNS))

        @block.gpsimd
        def _(pool):
            pool.memset(blank[:, :, 0:EF], 0.0).then_inc(blank_set, 1)
            pool.memset(blank[:, :, EF:RW], -1.0).then_inc(blank_set, 1)
            pool.wait_ge(blank_set, 2)
            for h in range(2):
                pool.dma_start(records[h * CHUNK * P:(h + 1) * CHUNK * P, :].rearrange("(p t) f -> p (t f)", t=CHUNK),
                               blank[:, :, :].rearrange("p t f -> p (t f)")).then_inc(moved[h], 16)
            pool.wait_ge(moved[0], 16)
            pool.wait_ge(moved[1], 16)
            pool.wait_ge(blanked, 32)
            with pool.Fori(0, GTURNS) as it:
                for h in range(2):
                    pool.wait_ge(rec_set, it * 2 + h + 1)
                    pool.wait_ge(rows_set, it * 2 + h + 1)
                    pool.sem_inc(pool_go, 1)
                    for g in range(GROUP):
                        pool.indirect_dma_start(
                            out=records[:, :],
                            out_offset=bass.IndirectOffsetOnAxis(ap=rowi[:, h, g:g + 1].bitcast(U32), axis=0),
                            in_=rec[:, h, g, :], in_offset=None).then_inc(moved[h], 16)
            pool.wait_ge(efmax_ready, 1)
            pool.partition_all_reduce(efmax[:, 1:2], efmax[:, 0:1], P, bass.bass_isa.ReduceOp.max).then_inc(efmax_all, 1)
            for h in range(2):
                pool.wait_ge(moved[h], 16 * GROUP * GTURNS + 16)
            with pool.Fori(0, CHUNKS // 2) as it:
                for h in range(2):
                    pool.wait_ge(recc_used[h], it + AHEAD)
                    pool.dma_start(recc[:, h, :, :].rearrange("p t f -> p (t f)"),
                                   records[ds((it * 2 + h) * (CHUNK * P), CHUNK * P), :]
                                   .rearrange("(p t) f -> p (t f)", p=P)).then_inc(recc_in[h], 16)
            with pool.Fori(0, L) as l:
                pool.wait_ge(mx_set, l + 1)
                pool.sem_inc(pool_go, 1)
                pool.partition_all_reduce(mxa[:, :], mx[:, :], P, bass.bass_isa.ReduceOp.max).then_inc(mx_all, 1)
                with pool.Fori(0, TURNS) as it:
                    pair0 = l * P0 + it * PAIRS
                    for q in range(PAIRS):
                        place = (q - 1) % RING
                        pool.wait_ge(mhi_set, pair0 + q + 1)
                        pool.tensor_tensor(m_lo[:, place, :], msg[:, place, :], m_hi[:, place, :], ALU.subtract)\
                            .then_inc(mlo_set, 1)

        @block.scalar
        def _(act):
            for s in (featT_set, o_set, x_set):
                act.sem_inc(s, AHEAD)
            for n in range(BANKS):
                w = WIDE[n][1]
                act.wait_ge(hT_ps, n + 1)
                act.activation(hT[:, n * BANK:n * BANK + w], sums[:, n * BANK:n * BANK + w], ACT.Copy).then_inc(hT_in, 1)
            act.wait_ge(s_ef, 16)
            act.wait_ge(dve_seq, LOC_STEP)
            with act.Fori(0, GTURNS) as it:
                for h in range(2):
                    col = it * (2 * GROUP) + h * GROUP
                    act.wait_ge(moved[h], it * (16 * GROUP) + 16)
                    act.activation(rec[:, h, :, 0:EF], big[:, ds(col * EF, GROUP * EF)]
                                   .rearrange("p (g f) -> p g f", f=EF), ACT.Copy)
                    act.activation(rec[:, h, :, EF:RW], loc[:, ds(col, GROUP), :], ACT.Copy).then_inc(rec_set, 1)
            act.wait_ge(scef_ready, 1)
            with act.Fori(0, CHUNKS // 2) as it:
                act.wait_ge(tr_done, it * 2 + AHEAD)
                for h in range(2):
                    act.wait_ge(recc_in[h], it * 16 + 16)
                    act.activation(stack[:, h, :, 0, :], recc[:, h, :, 0:EF], ACT.Copy, scale=sc_ef[:, 0:1])\
                       .then_inc(fhi_set, 1)
                for h in range(2):
                    act.wait_ge(tr_done, it * 2 + h + 1 + AHEAD)
                    act.wait_ge(feat_out[h], it * 16 + 16)
                    act.activation(featT[:, h, :], bank(h)[0:4 * EF, :].bitcast(F16), ACT.Copy).then_inc(featT_set, 1)
            with act.Fori(0, L) as l:
                act.wait_ge(w2t_ps, l + 1)
                act.activation(we2T[:, :], gath[:, 0:D], ACT.Copy).then_inc(w2t_set, 1)
                act.wait_ge(w21_ps, l + 1)
                act.activation(w21[:, :], gath[:, 0:D], ACT.Copy).then_inc(w21_set, 1)
                for s in range(AB_STEPS):
                    w = min(4 * D, (NB - 2 * s) * 2 * D)
                    act.wait_ge(ab_ps, l * AB_STEPS + s + 1)
                    act.activation(ab[:, s * 4 * D:s * 4 * D + w], bank(s % 6)[:, 0:w], ACT.Copy).then_inc(ab_set, 1)
                act.wait_ge(sc_set, l + 1)
                for s in range(T_PARTS):
                    b0, b1 = s * T_BLOCKS, (s + 1) * T_BLOCKS
                    act.activation(t_hi3[:, b0:b1, 0:2 * D], ab3[:, b0:b1, :], ACT.Copy, scale=sc[:, 0:1])\
                       .then_inc(thi_set, 1)
                with act.Fori(0, TURNS) as it:
                    pair0 = l * P0 + it * PAIRS
                    for q in range(PAIRS):
                        act.wait_ge(gath_done, pair0 + q + 1 + AHEAD)
                        act.wait_ge(mlo_set, pair0 + q + AHEAD)
                        act.activation(msg[:, q % RING, :], gath[:, :], ACT.Copy).then_inc(x_set, 1)
                        act.wait_ge(msg_set, pair0 + q + AHEAD)
                        act.wait_ge(sum_done, pair0 + q + AHEAD)
                        act.activation(m_hi[:, (q - 1) % RING, :], msg[:, (q - 1) % RING, :], ACT.Copy)\
                           .then_inc(mhi_set, 1)
                act.wait_ge(sum_done, (l + 1) * P0 + AHEAD)
                for n in range(BANKS):
                    w = WIDE[n][1]
                    act.activation(sumS[:, n * BANK:n * BANK + w], sums[:, n * BANK:n * BANK + w], ACT.Copy,
                                   scale=sc[:, 1:2]).then_inc(sums_out, 1)
                for n in range(BANKS):
                    w = WIDE[n][1]
                    act.wait_ge(z_ps, l * BANKS + n + 1)
                    act.activation(zbuf[:, n * BANK:n * BANK + w], sums[:, n * BANK:n * BANK + w], ACT.Copy)\
                       .then_inc(z_set, 1)
                for n in range(BANKS):
                    w = WIDE[n][1]
                    act.wait_ge(o_ps, l * BANKS + n + 1 + AHEAD)
                    act.wait_ge(h_set, l * BANKS + n + 1 + AHEAD)
                    act.activation(outT[:, n * BANK:n * BANK + w], sums[:, n * BANK:n * BANK + w], ACT.Copy)\
                       .then_inc(o_set, 1)
            act.wait_ge(var_set, 1)
            act.activation(rstd[:, :], rstd[:, :], ACT.Sqrt).then_inc(std_set, 1)

        @block.vector
        def _(dve):
            steps = [0]

            def then(ins):
                steps[0] += 1
                ins.then_inc(dve_seq, 1)
                dve.wait_ge(dve_seq, steps[0])

            def exponent(dst, field, shift_bits, sign):
                return dve.tensor_scalar(dst.bitcast(I32), field, float(sign), float(shift_bits * EXP1), ALU.mult, ALU.add)

            for s in (msg_set, hot_set, numT_set, h_set, mlo_set, recc_used[0], recc_used[1]):
                dve.sem_inc(s, AHEAD)
            dve.wait_ge(s_const, 16 * 6)
            dve.wait_ge(s_edges, 32)
            then(dve.tensor_tensor(lo_n[:, :], src_t[:, :], dst_t[:, :], ALU.min))
            then(dve.tensor_tensor(hi_n[:, :], src_t[:, :], dst_t[:, :], ALU.max))
            then(dve.tensor_scalar(lo_b, lo_n[:, :], 7, None, ALU.logical_shift_right))
            then(dve.tensor_scalar(hi_b, hi_n[:, :], 7, None, ALU.logical_shift_right))
            then(dve.tensor_scalar(src_t[:, :], lo_n[:, :], P - 1, None, ALU.bitwise_and))
            then(dve.tensor_scalar(dst_t[:, :], hi_n[:, :], P - 1, None, ALU.bitwise_and))
            then(dve.tensor_scalar(key[:, :], hi_b, float(NB), float(-DEAD), ALU.is_equal, ALU.mult))
            then(dve.tensor_tensor(loc[:, :, 0], src_t[:, :], key[:, :], ALU.add))
            then(dve.tensor_tensor(loc[:, :, 1], dst_t[:, :], key[:, :], ALU.add))
            then(dve.tensor_copy(ident16[:, :], ident[:, :]))
            then(dve.memset(zeros[:, :], 0.0))
            then(dve.memset(zeros16[:, :], 0.0))
            assert steps[0] == LOC_STEP
            then(dve.scalar_tensor_tensor(key[:, :], hi_b, 1.0, hi_b, ALU.add, ALU.mult))
            then(dve.scalar_tensor_tensor(key[:, :], key[:, :], 0.5, lo_b, ALU.mult, ALU.add))

            def keys(it, after):
                dve.wait_ge(hot_set, it * (2 * GROUP) + after * (2 * GROUP) + AHEAD)
                dve.tensor_copy(keyc[:, :], key[:, ds(it * (2 * GROUP), 2 * GROUP)]).then_inc(keyc_set, 1)
                dve.wait_ge(keyc_set, after + it + 1)

            def one_hot(k):
                dve.tensor_scalar(onehot[:, k, :], iota[:, 0:BUCKETS], keyc[:, k:k + 1], None, ALU.is_equal)\
                   .then_inc(hot_set, 1)

            with dve.Fori(0, GTURNS) as it:
                keys(it, 0)
                dve.wait_ge(hist_half, it * 2 + AHEAD)
                for h in range(2):
                    for g in range(GROUP):
                        one_hot(h * GROUP + g)
            dve.wait_ge(hist_half, 2 * GTURNS + AHEAD)
            then(dve.tensor_copy(cnt_i[:, :], bank(0)[:, 0:BUCKETS]))
            then(dve.tensor_scalar(cnt_i[:, :], cnt_i[:, :], float(P - 1), None, ALU.add))
            then(dve.tensor_scalar(cnt_i[:, :], cnt_i[:, :], 7, None, ALU.logical_shift_right))
            then(dve.tensor_copy(cnt_f[:, :], cnt_i[:, :]))
            then(dve.tensor_tensor_scan(tile_end[:, :], cnt_f[:, :], zeros[:, :], 0.0, ALU.add, ALU.add))
            dve.tensor_tensor(tile_beg[:, :], tile_end[:, :], cnt_f[:, :], ALU.subtract).then_inc(beg_ready, 1)
            for q in range(MAPQ):
                for s in range(2):
                    then(dve.scalar_tensor_tensor(scrap[:, :], tile_end[:, :], tiles_c[:, q:q + 1], steps_c[:, s, :],
                                                  ALU.is_le, ALU.mult, accum_out=map_f[:, q, s:s + 1]))
            dve.tensor_copy(map_i[:, :, :], map_f[:, :, :]).then_inc(map_ready, 1)
            with dve.Fori(0, GTURNS) as it:
                keys(it, GTURNS)
                for h in range(2):
                    one_hot(h * GROUP)
                    for g in range(GROUP):
                        if g + 1 < GROUP:
                            one_hot(h * GROUP + g + 1)
                        dve.wait_ge(rank_set, it * (2 * GROUP) + (h * GROUP + g + 1))
                        dve.scalar_tensor_tensor(scrap[:, :], bank(1)[:, 0:BUCKETS], 1.0, onehot[:, h * GROUP + g, :],
                                                 ALU.mult, ALU.mult, accum_out=slot_f[:, g:g + 1]).then_inc(rank_read, 1)
                    row0 = it * 10 + h * 5
                    dve.wait_ge(rank_read, it * (2 * GROUP) + (h + 1) * GROUP)
                    dve.tensor_copy(slot_i[:, :], slot_f[:, :]).then_inc(rows_seq, 1)
                    dve.wait_ge(rows_seq, row0 + 1)
                    dve.tensor_scalar(rowa[:, :], slot_i[:, :], P - 1, 3, ALU.bitwise_and, ALU.logical_shift_left)\
                       .then_inc(rows_seq, 1)
                    dve.wait_ge(rows_seq, row0 + 2)
                    dve.tensor_scalar(rowb[:, :], slot_i[:, :], 7, CHUNK - 1, ALU.logical_shift_right, ALU.bitwise_and)\
                       .then_inc(rows_seq, 1)
                    dve.wait_ge(rows_seq, row0 + 3)
                    dve.tensor_tensor(rowa[:, :], rowa[:, :], rowb[:, :], ALU.bitwise_or).then_inc(rows_seq, 1)
                    dve.wait_ge(rows_seq, row0 + 4)
                    dve.tensor_scalar(slot_i[:, :], slot_i[:, :], 10, 10, ALU.logical_shift_right, ALU.logical_shift_left)\
                       .then_inc(rows_seq, 1)
                    dve.wait_ge(rows_seq, row0 + 5)
                    dve.wait_ge(moved[h], it * (16 * GROUP) + 16)
                    dve.tensor_tensor(rowi[:, h, :], rowa[:, :], slot_i[:, :], ALU.bitwise_or).then_inc(rows_set, 1)
            dve.wait_ge(s_ef, 16)
            dve.tensor_reduce(efmax[:, 0:1], big[:, :], AX_X, ALU.max, apply_absolute_value=True).then_inc(efmax_ready, 1)
            dve.wait_ge(efmax_all, 1)
            then(dve.tensor_scalar(bnd[:, 0:1], efmax[:, 1:2], 2.0 ** -100, None, ALU.max))
            then(dve.tensor_scalar(ebits[:, 0:1], bnd[:, 0:1].bitcast(I32), EXP_MASK, None, ALU.bitwise_and))
            then(exponent(sc_ef[:, 0:1], ebits[:, 0:1], 259, -1))
            exponent(sc_ef[:, 1:2], ebits[:, 0:1], -5, 1).then_inc(scef_ready, 1)
            dve.wait_ge(scef_ready, 1)
            with dve.Fori(0, CHUNKS // 2) as it:
                for h in range(2):
                    c = it * 2 + h
                    dve.wait_ge(recc_in[h], it * 16 + 16)
                    dve.tensor_copy(numcol[:, ds(c * (2 * CHUNK), 2 * CHUNK)].rearrange("p (t s) -> p t s", s=2),
                                    recc[:, h, :, EF:RW])
                    dve.wait_ge(tr_done, it * 2 + AHEAD)
                    dve.tensor_copy(num16[:, h, :].rearrange("p (t s) -> p t s", s=2), recc[:, h, :, EF:RW])
                    dve.wait_ge(fhi_set, c + 1)
                    dve.scalar_tensor_tensor(stack[:, h, :, 1, :], recc[:, h, :, 0:EF], sc_ef[:, 0:1],
                                             stack[:, h, :, 0, :], ALU.mult, ALU.subtract).then_inc(recc_used[h], 1)
                    dve.wait_ge(recc_used[h], it + 1 + AHEAD)
                    dve.tensor_copy(stack[:, h, :, 2:4, :], stack[:, h, :, 0:2, :]).then_inc(fst_set, 1)
                for h in range(2):
                    dve.wait_ge(tr_done, it * 2 + h + 1 + AHEAD)
                    dve.wait_ge(nums_out[h], it * 16 + 16)
                    dve.tensor_copy(numT[:, h, :], bank(2 + h)[0:2 * CHUNK, 0:P // 2].bitcast(F16)).then_inc(numT_set, 1)
            then(dve.memset(ssel[:, ITER - 2 * LAG:ITER, :, :], 0.0))
            then(dve.memset(mx[:, :], 0.0))
            dve.memset(msg[:, RING - 1, :], 0.0)
            dve.memset(m_hi[:, RING - LAG:RING, :], 0.0)
            dve.memset(m_lo[:, RING - LAG:RING, :], 0.0).then_inc(mlo_set, 1)

            def leaky(m):
                return dve.scalar_tensor_tensor(m, m, SLOPE, m, ALU.mult, ALU.max)

            def gather_one_hot(h, c):
                dve.tensor_scalar(gsel[:, h, :], numb[:, h, :], part[:, 0:1], None, ALU.is_equal).then_inc(gsel_set, 1)

            dve.wait_ge(numb_in[0], 16)
            gather_one_hot(0, 0)
            with dve.Fori(0, L) as l:
                dve.wait_ge(w_in, (l + 1) * (16 * W_DMAS))
                dve.tensor_reduce(mx[0:4 * EF, 1:2], wc[:, :], AX_X, ALU.max, apply_absolute_value=True)
                for s in range(AB_STEPS):
                    w = min(4 * D, (NB - 2 * s) * 2 * D)
                    dve.wait_ge(ab_set, l * AB_STEPS + s + 1)
                    dve.tensor_reduce(abmax[:, s:s + 1], ab[:, s * 4 * D:s * 4 * D + w], AX_X, ALU.max,
                                      apply_absolute_value=True).then_inc(ab_maxed, 1)
                dve.wait_ge(ab_maxed, (l + 1) * AB_STEPS)
                dve.tensor_reduce(mx[:, 0:1], abmax[:, 0:AB_STEPS], AX_X, ALU.max).then_inc(mx_set, 1)
                dve.memset(sums[:, 0:NODES], 0.0).then_inc(sums_zero, 1)
                dve.wait_ge(mx_all, l + 1)
                seq = l * 6
                dve.tensor_tensor(bnd[:, 0:1], mxa[:, 1:2], efmax[:, 1:2], ALU.mult)\
                   .then_inc(sc_seq, 1)
                dve.tensor_scalar(bnd[:, 1:2], mxa[:, 0:1], 2.0, 2.0 ** -100, ALU.mult, ALU.max).then_inc(sc_seq, 1)
                dve.wait_ge(sc_seq, seq + 2)
                dve.scalar_tensor_tensor(bnd[:, 0:1], bnd[:, 0:1], float(EF), bnd[:, 1:2], ALU.mult, ALU.add)\
                   .then_inc(sc_seq, 1)
                dve.wait_ge(sc_seq, seq + 3)
                dve.tensor_scalar(ebits[:, 0:1], bnd[:, 0:1].bitcast(I32), EXP_MASK, None, ALU.bitwise_and)\
                   .then_inc(sc_seq, 1)
                dve.wait_ge(sc_seq, seq + 4)
                exponent(sc[:, 0:1], ebits[:, 0:1], 268, -1).then_inc(sc_seq, 1)
                dve.wait_ge(sc_seq, seq + 5)
                exponent(sc[:, 1:2], ebits[:, 0:1], -14, 1).then_inc(sc_set, 1)
                dve.tensor_scalar(sc_w[:, :], sc[:, 0:1], sc_ef[:, 1:2], 2.0 ** 120, ALU.mult, ALU.min).then_inc(sc_seq, 1)
                dve.wait_ge(sc_seq, seq + 6)
                wseq = l * 4
                dve.tensor_scalar(wcs[:, :], wc[:, :], sc_w[0:4 * EF, 0:1], None, ALU.mult).then_inc(wst_set, 1)
                dve.wait_ge(wst_set, wseq + 1)
                dve.tensor_copy(wch[:, :], wcs[:, :]).then_inc(wst_set, 1)
                dve.wait_ge(wst_set, wseq + 2)
                for k in range(2):
                    dve.tensor_copy(wst[0:2 * EF, k, :], wch[0:2 * EF, :])
                    last = dve.tensor_tensor(wst[2 * EF:4 * EF, k, :], wcs[2 * EF:4 * EF, :], wch[2 * EF:4 * EF, :],
                                             ALU.subtract)
                    last.then_inc(wst_set, 1)
                for s in range(T_PARTS):
                    b0, b1 = s * T_BLOCKS, (s + 1) * T_BLOCKS
                    dve.wait_ge(thi_set, l * T_PARTS + s + 1)
                    dve.tensor_copy(t_hi3[:, b0:b1, 2 * D:3 * D], t_hi3[:, b0:b1, 0:D])
                    dve.scalar_tensor_tensor(t_lo3[:, b0:b1, 0:2 * D], ab3[:, b0:b1, :], sc[:, 0:1],
                                             t_hi3[:, b0:b1, 0:2 * D], ALU.mult, ALU.subtract).then_inc(tables_set, 1)
                dve.wait_ge(tables_set, l * (T_PARTS + 1) + T_PARTS)
                dve.tensor_copy(t_lo3[:, :, 2 * D:3 * D], t_lo3[:, :, 0:D]).then_inc(tables_set, 1)
                with dve.Fori(0, TURNS) as it:
                    pair0 = l * P0 + it * PAIRS
                    turn = l * TURNS + it
                    dve.wait_ge(msg_set, pair0 + AHEAD)
                    dve.tensor_copy(numc[:, :], numcol[:, ds(it * (2 * ITER), 2 * ITER)]).then_inc(numc_set, 1)
                    dve.wait_ge(numc_set, turn + 1)
                    for q in range(PAIRS):
                        for t in (2 * q, 2 * q + 1):
                            for s in range(2):
                                dve.tensor_scalar(ssel[:, t, s, :], iota[:, 0:P], numc[:, 2 * t + s:2 * t + s + 1], None,
                                                  ALU.is_equal)
                        dve.wait_ge(x_set, pair0 + q + 1 + AHEAD)
                        leaky(msg[:, q % RING, :]).then_inc(msg_set, 1)
                        if q % 4 == 1:
                            h = q // 4
                            chunk = it * 2 + h
                            dve.wait_ge(gath_done, l * P0 + chunk * (CHUNK // 2) + AHEAD)
                            dve.wait_ge(numb_in[1 - h], turn * 16 + (32 if h else 16))
                            gather_one_hot(1 - h, None)
                for n in range(BANKS):
                    w = WIDE[n][1]
                    dve.wait_ge(z_set, l * BANKS + n + 1)
                    leaky(zbuf[:, n * BANK:n * BANK + w]).then_inc(zl_set, 1)
                for n in range(BANKS):
                    w = WIDE[n][1]
                    part_n = slice(n * BANK, n * BANK + w)
                    dve.wait_ge(o_ps, l * BANKS + n + 1 + AHEAD)
                    dve.tensor_tensor(hT[:, part_n], hT[:, part_n], sums[:, part_n], ALU.add).then_inc(h_set, 1)
            for n in range(YSTEPS):
                b0, b1 = 4 * n, min(4 * n + 4, NB)
                w = (b1 - b0) * D
                dve.wait_ge(y_ps, n + 1)
                dve.tensor_tensor(y[:, b0:b1, :].rearrange("p b f -> p (b f)"), sums[:, n * BANK:n * BANK + w],
                                  xn[:, b0:b1, :].rearrange("p b f -> p (b f)"), ALU.add).then_inc(y_seq, 1)
            dve.wait_ge(y_seq, YSTEPS)
            for b in range(NB):
                dve.bn_stats(stats[:, b, :], y[:, b, :]).then_inc(y_seq, 1)
            dve.wait_ge(y_seq, YSTEPS + NB)
            for b in range(NB):
                dve.bn_aggr(mv[:, b, :], stats[:, b, :]).then_inc(y_seq, 1)
            dve.wait_ge(y_seq, YSTEPS + 2 * NB)
            dve.tensor_scalar(rstd[:, :], mv[:, :, 1], 1e-5, None, ALU.add).then_inc(var_set, 1)
            dve.wait_ge(std_set, 1)
            dve.reciprocal(rstd[:, :], rstd[:, :]).then_inc(y_seq, 1)
            dve.wait_ge(y_seq, YSTEPS + 2 * NB + 1)
            for b in range(NB):
                last = dve.tensor_scalar(y[:, b, :], y[:, b, :], mv[:, b, 0:1], rstd[:, b:b + 1], ALU.subtract, ALU.mult)
            last.then_inc(y_set, 1)

        @block.tensor
        def _(pe):
            for s in (gath_done, tr_done, sum_done, hist_half, o_ps):
                pe.sem_inc(s, AHEAD)
            pe.wait_ge(s_const, 16 * 6)
            pe.wait_ge(s_x, 16)
            for b in range(NB):
                last = pe.transpose(sums[:, b * P:(b + 1) * P], xn[:, b, :], ident[:, :])
                if b % 4 == 3 or b == NB - 1:
                    last.then_inc(hT_ps, 1)
            pe.wait_ge(hT_in, BANKS)
            hist = bank(0)[:, 0:BUCKETS]
            pe.wait_ge(dve_seq, LOC_STEP)
            pe.matmul(hist, tri[:, 2, :], zeros16[:, :], start=True, stop=False, skip_group_check=True)
            with pe.Fori(0, GTURNS) as it:
                for h in range(2):
                    for g in range(GROUP):
                        pe.wait_ge(hot_set, it * (2 * GROUP) + (h * GROUP + g + 1) + AHEAD)
                        last = pe.matmul(hist, tri[:, 2, :], onehot[:, h * GROUP + g, :], start=False, stop=False,
                                         skip_group_check=True)
                    last.then_inc(hist_half, 1)
            pe.wait_ge(beg_ready, 1)
            rank = bank(1)[:, 0:BUCKETS]
            pe.matmul(rank, tri[:, 2, :], tile_beg[:, :], start=True, stop=False, skip_group_check=True)
            with pe.Fori(0, GTURNS) as it:
                for k in range(2 * GROUP):
                    pe.wait_ge(hot_set, it * (2 * GROUP) + (COLS + k + 1) + AHEAD)
                    pe.matmul(rank, tri[:, 0, :], onehot[:, k, :], start=False, stop=False, skip_group_check=True)\
                      .then_inc(rank_set, 1)
                    pe.wait_ge(rank_read, it * (2 * GROUP) + (k + 1))
                    pe.matmul(rank, tri[:, 1, :], onehot[:, k, :], start=False, stop=False, skip_group_check=True)
            with pe.Fori(0, CHUNKS // 2) as it:
                for h in range(2):
                    pe.wait_ge(dve_seq, LOC_STEP)
                    pe.wait_ge(fst_set, it * 2 + h + 1)
                    pe.wait_ge(featT_set, it * 2 + AHEAD)
                    pe.wait_ge(numT_set, it * 2 + AHEAD)
                    pe.sem_inc(pe_go, 1)
                    for t in range(CHUNK):
                        pe.transpose(bank(h)[0:4 * EF, t * P // 2:(t + 1) * P // 2].bitcast(F16),
                                     stack[:, h, t, :, :].rearrange("p k f -> p (k f)"), ident16[:, :])
                    pe.transpose(bank(2 + h)[0:2 * CHUNK, 0:P // 2].bitcast(F16), num16[:, h, :], ident16[:, :])\
                      .then_inc(tr_done, 1)
            with pe.Fori(0, L) as l:
                pe.wait_ge(w_in, (l + 1) * (16 * W_DMAS))
                pe.transpose(gath[:, 0:D], we2[:, :], ident[:, :]).then_inc(w2t_ps, 1)
                pe.wait_ge(w2t_set, l + 1)
                pe.matmul(gath[:, 0:D], we2T[:, :], wn1[:, 1, :], start=True, stop=True).then_inc(w21_ps, 1)
                pe.wait_ge(h_set, l * BANKS + AHEAD)
                pe.wait_ge(o_set, l * BANKS + AHEAD)
                for s in range(AB_STEPS):
                    if s >= 6:
                        pe.wait_ge(ab_set, l * AB_STEPS + s - 5)
                    for b in range(2 * s, min(2 * s + 2, NB)):
                        last = pe.matmul(bank(s % 6)[:, (b % 2) * 2 * D:(b % 2 + 1) * 2 * D], hT[:, b * P:(b + 1) * P],
                                         wab[:, :, :].rearrange("p s f -> p (s f)"), start=True, stop=True)
                    last.then_inc(ab_ps, 1)
                pe.wait_ge(w21_set, l + 1)
                pe.wait_ge(tables_set, (l + 1) * (T_PARTS + 1))
                pe.wait_ge(map_in, 16)
                pe.wait_ge(wst_set, (l + 1) * 4)
                pe.wait_ge(sums_zero, l + 1)
                pe.sem_inc(pe_go, 1)
                with pe.Fori(0, TURNS) as it:
                    pair0 = l * P0 + it * PAIRS
                    turn = l * TURNS + it

                    def blocks(first, n):
                        _, v = nc.values_load_multi_w_load_instructions(
                            map_row[0:1, ds(it * (2 * ITER) + 2 * (first + PADDED_MAP), 2 * n)],
                            engines=(mybir.EngineType.PE,), min_val=0, max_val=NB - 1,
                            skip_runtime_bounds_check_because="sums of the constant steps over the first buckets")
                        return {first + t: (v[2 * t], v[2 * t + 1]) for t in range(n)}

                    for q in range(PAIRS):
                        h = q // 4
                        if q % 4 == 0:
                            of_tile = blocks(2 * q - 2 * LAG, 2 * LAG + CHUNK)
                        if q % 4 == 0:
                            pe.wait_ge(gsel_set, turn * 2 + h + 1)
                            pe.wait_ge(fchunk_in[h], turn * 16 + 16)
                        pe.wait_ge(x_set, pair0 + q + AHEAD)
                        for i in range(2):
                            t = 2 * q + i
                            tc = t % CHUNK
                            b0, b1 = of_tile[t]
                            uv = gath[:, i * 2 * D:(i + 1) * 2 * D]
                            at_lo = gsel[:, h, 2 * tc * P:(2 * tc + 1) * P]
                            at_hi = gsel[:, h, (2 * tc + 1) * P:(2 * tc + 2) * P]
                            pe.matmul(uv, fchunk[:, h, tc * P:(tc + 1) * P], wst[:, :, :].rearrange("p s f -> p (s f)"),
                                      start=True, stop=False, skip_group_check=True)
                            pe.matmul(uv, at_lo, t_hi[:, ds(b0 * TW, 2 * D)], start=False, stop=False, skip_group_check=True)
                            pe.matmul(uv, at_lo, t_lo[:, ds(b0 * TW, 2 * D)], start=False, stop=False, skip_group_check=True)
                            pe.matmul(uv, at_hi, t_hi[:, ds(b1 * TW + D, 2 * D)], start=False, stop=False,
                                      skip_group_check=True)
                            last = pe.matmul(uv, at_hi, t_lo[:, ds(b1 * TW + D, 2 * D)], start=False, stop=True,
                                             skip_group_check=True)
                        last.then_inc(gath_done, 1)
                        pe.wait_ge(mlo_set, pair0 + q + AHEAD)
                        place = (q - LAG) % RING
                        for i in range(2):
                            t = 2 * (q - LAG) + i
                            b0, b1 = of_tile[t]
                            for s, b in ((1, b1), (0, b0)):
                                w0 = i * 2 * D + (1 - s) * D
                                for m in (m_hi, m_lo):
                                    last = pe.matmul(sums[:, ds(b * P, P)], m[:, place, w0:w0 + D],
                                                     ssel[:, t % ITER, s, :], start=False, stop=False,
                                                     skip_group_check=True)
                        last.then_inc(sum_done, 1)
                for n in range(BANKS):
                    w = WIDE[n][1]
                    cols = slice(n * BANK, n * BANK + w)
                    pe.wait_ge(sums_out, l * BANKS + n + 1)
                    pe.matmul(sums[:, cols], wn1[:, 0, :], hT[:, cols], start=True, stop=False)
                    pe.matmul(sums[:, cols], w21[:, :], sumS[:, cols], start=False, stop=True).then_inc(z_ps, 1)
                for n in range(BANKS):
                    w = WIDE[n][1]
                    cols = slice(n * BANK, n * BANK + w)
                    pe.wait_ge(zl_set, l * BANKS + n + 1)
                    pe.matmul(sums[:, cols], wn2[:, :], zbuf[:, cols], start=True, stop=True).then_inc(o_ps, 1)
            for n in range(YSTEPS):
                b0, b1 = 4 * n, min(4 * n + 4, NB)
                pe.wait_ge(o_set, L * BANKS + AHEAD)
                for b in range(b0, b1):
                    last = pe.transpose(sums[:, b * P:(b + 1) * P], outT[:, b * P:(b + 1) * P], ident[:, :])
                last.then_inc(y_ps, 1)


def constants(np):
    i = np.arange(P)
    earlier = (i[:, None] < i[None, :]).astype(np.float16)
    tri = np.stack([earlier, 1 - earlier, np.ones_like(earlier)], axis=1)
    lo = [b for a in range(NB) for b in range(a + 1)] + [0, 0]
    hi = [a for a in range(NB) for b in range(a + 1)] + [0, 0]
    steps = np.stack([np.diff(lo), np.diff(hi)]).astype(np.float32)
    tiles = (np.arange(MAPQ)[None, :] * P + i[:, None] - 2 * LAG).astype(np.float32)
    return {
        "c_iota": np.ascontiguousarray(np.broadcast_to(np.arange(384, dtype=np.float16), (P, 384))),
        "c_part": i.astype(np.float32).reshape(P, 1),
        "c_tri": np.ascontiguousarray(tri),
        "c_ident": np.eye(P, dtype=np.float32),
        "c_tiles": np.ascontiguousarray(tiles),
        "c_steps": np.ascontiguousarray(np.broadcast_to(steps, (P, 2, BUCKETS))),
    }


def kernel(x, src, dst, edge_attr_16, L0_gnn_We1, L0_gnn_We2, L0_gnn_Wn1, L0_gnn_Wn2):
    import numpy as np
    import concourse.bacc as bacc
    from concourse.bass_utils import run_bass_kernel_spmd

    def padded(a, rows, fill):
        a = np.asarray(a)
        whole = np.full((rows,) + a.shape[1:], fill, a.dtype)
        whole[:a.shape[0]] = a
        return whole

    arrays = {
        "x": padded(x, NODES, 0),
        "src": padded(src, P * COLS, 0),
        "dst": padded(dst, P * COLS, NODES),
        "ef": padded(edge_attr_16, P * COLS, 0),
        "We1": np.ascontiguousarray(L0_gnn_We1),
        "We2": np.ascontiguousarray(L0_gnn_We2),
        "Wn1": np.ascontiguousarray(L0_gnn_Wn1),
        "Wn2": np.ascontiguousarray(L0_gnn_Wn2),
        **constants(np),
    }
    nc = bacc.Bacc("TRN2", target_bir_lowering=False, num_devices=1)
    args = {k: nc.dram_tensor(k, a.shape, mybir.dt.from_np(a.dtype), kind="ExternalInput").ap() for k, a in arrays.items()}
    out = nc.dram_tensor("out", (N, D), F32, kind="ExternalOutput").ap()
    build(nc, **args, out=out)
    r = run_bass_kernel_spmd(nc, [arrays], core_ids=[0])
    return r.results[0]["out"]
```

```python
from contextlib import ExitStack

import concourse.bass as bass
from concourse import mybir

P = 128
N, E, D, EF, L = 3125, 100000, 128, 16, 3
NB = -(-N // P)
NODES = NB * P
COLS = 784
PADS = P * COLS - E
BUCKETS = NB * (NB + 1) // 2 + 1
CHUNK = 8
STEP = 3
STEPS = 8
LAG = 3
ITER = STEPS * STEP
HALF = ITER // 2
TILES = 1128
LIVE_BOUND = (E + (BUCKETS - 1) * (P - 1)) // P + -(-PADS // P)
assert LIVE_BOUND + STEP * LAG <= TILES and TILES % ITER == 0
CHUNKS = TILES // CHUNK
TURNS = TILES // ITER
PREP = 3
assert CHUNKS % PREP == 0
RING = 4
MSG = STEP * 2 * D
RW = EF + 2
GROUP = 14
GTURNS = COLS // (2 * GROUP)
MAPQ = -(-(TILES + STEP * LAG) // P)
PLANES = 3
BANK = 512
BANKS = -(-NODES // BANK)
AHEAD = 1
SLOPE = 0.01
DEAD = 1000
EXP_MASK = 0x7F800000
EXP1 = 1 << 23

ALU = mybir.AluOpType
ACT = mybir.ActivationFunctionType
F32 = mybir.dt.float32
F16 = mybir.dt.float16
I32 = mybir.dt.int32
U32 = mybir.dt.uint32
AX_X = mybir.AxisListType.X
ds = bass.DynSlice


def build(nc, x, src, dst, ef, We1, We2, Wn1, Wn2, c_iota, c_part, c_tri, c_ident, c_tiles, c_steps, out):
    records = nc.dram_tensor("records", [TILES * P, RW], F32)
    feat_d = nc.dram_tensor("feat_d", [4 * EF, (TILES + HALF) * P], F16)
    nums_d = nc.dram_tensor("nums_d", [(TILES + HALF) * 2, P], F16)
    map_d = nc.dram_tensor("map_d", [MAPQ * P, 2], I32)

    with ExitStack() as ctx:
        def sb(name, shape, dt):
            return ctx.enter_context(nc.sbuf_tensor(name, shape, dt))

        def sem(name):
            return ctx.enter_context(nc.semaphore(name))

        sums = ctx.enter_context(nc.psum_tensor("sums", [P, BANKS * BANK], F32))
        gath = ctx.enter_context(nc.psum_tensor("gath", [P, BANK], F32))

        def bank(n):
            return sums[:, n * BANK:(n + 1) * BANK]

        gath6 = sums[:, BANKS * BANK - 2 * D:BANKS * BANK]

        loop_words = (ITER * 2 * P + 2 * RING * MSG) // 2
        loop_buf = sb("loop_buf", [P, loop_words], F32)
        ssel_words, m_words = ITER * P, RING * MSG // 2
        ssel = loop_buf[:, 0:ssel_words].bitcast(F16).rearrange("p (t s e) -> p t s e", s=2, e=P)
        m_hi = loop_buf[:, ssel_words:ssel_words + m_words].bitcast(F16).rearrange("p (r f) -> p r f", r=RING)
        m_lo = loop_buf[:, ssel_words + m_words:loop_words].bitcast(F16).rearrange("p (r f) -> p r f", r=RING)
        x0 = loop_buf[:, 0:NODES].rearrange("p (b f) -> p b f", f=D)
        taken = [NODES]

        def early(words):
            taken[0] += words
            assert taken[0] <= loop_words
            return loop_buf[:, taken[0] - words:taken[0]]

        def planes_of(ps):
            return ps.rearrange("p (k n) -> p k n", k=2)

        iota = sb("iota", [P, 384], F16)
        part = sb("part", [P, 1], F32)
        tri = sb("tri", [P, 3, P], F16)
        ident = sb("ident", [P, P], F32)
        ident16 = sb("ident16", [P, P], F16)
        tiles_c = sb("tiles_c", [P, MAPQ], F32)
        steps_c = early(2 * BUCKETS).rearrange("p (s b) -> p s b", s=2)
        big = sb("big", [P, max(COLS * EF, 3 * NODES + RING * MSG)], F32)
        ef_t = big[:, 0:COLS * EF]
        t_hi = sb("t_hi", [P, PLANES * NODES], F16)
        t_lo = sb("t_lo", [P, PLANES * NODES], F16)
        t_hi_words = t_hi[:, :].bitcast(F32)
        src_t, dst_t, lo_n, hi_n, lo_b, hi_b = (t_hi_words[:, k * COLS:(k + 1) * COLS].bitcast(I32) for k in range(6))
        onehot = t_lo[:, 0:2 * GROUP * BUCKETS].rearrange("p (g b) -> p g b", b=BUCKETS)
        numb = sb("numb", [P, 2, HALF * 2 * P], F16)
        gsel = sb("gsel", [P, 2, HALF * 2 * P], F16)
        fchunk = sb("fchunk", [4 * EF, 2, HALF * P], F16)
        loc = numb[:, :, :].rearrange("p h e -> p (h e)").bitcast(F32)[:, 0:2 * COLS]\
            .rearrange("p (j s) -> p j s", s=2)
        key = gsel[:, :, :].rearrange("p h e -> p (h e)").bitcast(F32)[:, 0:COLS]
        featT = fchunk[:, :, :].rearrange("p h e -> p (h e)").rearrange("p (h e) -> p h e", h=PREP)
        keyc = sb("keyc", [P, 2 * GROUP], F32)
        scrap = early(BUCKETS)
        cnt_i = early(BUCKETS).bitcast(I32)
        cnt_f = early(BUCKETS)
        tile_end = early(BUCKETS)
        tile_beg = early(BUCKETS // 2).bitcast(F16)
        zeros = early(BUCKETS)
        zeros16 = early(BUCKETS // 2).bitcast(F16)
        map_f = sb("map_f", [P, MAPQ, 2], F32)
        map_i = sb("map_i", [P, MAPQ, 2], I32)
        map_row = sb("map_row", [1, MAPQ * P * 2], I32)
        slot_f = sb("slot_f", [P, GROUP], F32)
        slot_i = sb("slot_i", [P, GROUP], I32)
        rowa = sb("rowa", [P, GROUP], I32)
        rowb = sb("rowb", [P, GROUP], I32)
        rowi = sb("rowi", [P, 2, GROUP], I32)
        rec = sb("rec", [P, 2, GROUP, RW], F32)
        blank = sb("blank", [P, CHUNK, RW], F32)
        recc = sb("recc", [P, PREP, CHUNK, RW], F32)
        stack = sb("stack", [P, PREP, CHUNK, 4, EF], F16)
        num16 = sb("num16", [P, PREP, CHUNK * 2], F16)
        numT = sb("numT", [2 * CHUNK, PREP, P], F16)
        numcol = sb("numcol", [P, TILES * 2], F16)
        hT = sb("hT", [P, NODES], F32)
        xn = t_hi_words[:, 0:NODES].rearrange("p (b f) -> p b f", f=D)
        ab = big[:, 0:NB * 2 * D]
        ab3 = ab.rearrange("p (k n) -> p k n", k=2)

        def two_planes(t, b0, b1):
            return t[:, 0:2 * NODES].rearrange("p (k n) -> p k n", k=2)[:, :, b0 * P:b1 * P]

        sumS = big[:, 0:NODES]
        zbuf = big[:, NODES:2 * NODES]
        outT = big[:, 2 * NODES:3 * NODES]
        y = big[:, 0:NODES].rearrange("p (b f) -> p b f", f=D)
        msg = big[:, 3 * NODES:3 * NODES + RING * MSG].rearrange("p (r f) -> p r f", r=RING)
        wab = sb("wab", [P, 2, D], F32)
        wc = sb("wc", [4 * EF, D], F32)
        wcs = sb("wcs", [4 * EF, D], F32)
        wch = sb("wch", [4 * EF, D], F16)
        wst = sb("wst", [4 * EF, 2, D], F16)
        we2 = sb("we2", [P, D], F32)
        we2T = sb("we2T", [P, D], F32)
        wn1 = sb("wn1", [P, 2, D], F32)
        w21 = sb("w21", [P, D], F32)
        wn2 = sb("wn2", [P, D], F32)
        efmax = sb("efmax", [P, 2], F32)
        sc_ef = sb("sc_ef", [P, 2], F32)
        abmax = sb("abmax", [P, 16, 2], F32)
        mx = sb("mx", [P, 2], F32)
        mxa = sb("mxa", [P, 2], F32)
        bnd = sb("bnd", [P, 2], F32)
        sc = sb("sc", [P, 2], F32)
        sc_w = sb("sc_w", [P, 1], F32)
        ebits = sb("ebits", [P, 2], I32)
        numc = sb("numc", [P, ITER * 2], F32)
        stats = sb("stats", [P, NB, 6], F32)
        mv = sb("mv", [P, NB, 2], F32)
        rstd = sb("rstd", [P, NB], F32)

        s_const = sem("s_const")
        s_edges = sem("s_edges")
        s_ef = sem("s_ef")
        s_x = sem("s_x")
        blank_set = sem("blank_set")
        blanked = sem("blanked")
        dve_seq = sem("dve_seq")
        id16_ready = sem("id16_ready")
        efmax_ready = sem("efmax_ready")
        efmax_all = sem("efmax_all")
        scef_ready = sem("scef_ready")
        hT_ps = sem("hT_ps")
        hT_in = sem("hT_in")
        keyc_set = sem("keyc_set")
        hot_set = sem("hot_set")
        hist_half = sem("hist_half")
        beg_ready = sem("beg_ready")
        map_ready = sem("map_ready")
        map_out = sem("map_out")
        map_in = sem("map_in")
        rank_set = sem("rank_set")
        rank_read = sem("rank_read")
        rows_seq = sem("rows_seq")
        rows_set = sem("rows_set")
        rec_set = sem("rec_set")
        moved = [sem(f"moved{h}") for h in range(2)]
        recc_in = [sem(f"recc_in{h}") for h in range(PREP)]
        recc_used = [sem(f"recc_used{h}") for h in range(PREP)]
        fhi_set = sem("fhi_set")
        flo_set = sem("flo_set")
        fst_set = sem("fst_set")
        tr_done = sem("tr_done")
        featT_set = sem("featT_set")
        numT_set = sem("numT_set")
        feat_out = [sem(f"feat_out{h}") for h in range(PREP)]
        nums_out = [sem(f"nums_out{h}") for h in range(PREP)]
        wrap_out = sem("wrap_out")
        w_in = sem("w_in")
        w2t_ps = sem("w2t_ps")
        w2t_set = sem("w2t_set")
        w21_ps = sem("w21_ps")
        w21_set = sem("w21_set")
        ab_ps = sem("ab_ps")
        ab_set = sem("ab_set")
        ab_maxed = sem("ab_maxed")
        mx_set = sem("mx_set")
        mx_all = sem("mx_all")
        sc_seq = sem("sc_seq")
        sc_set = sem("sc_set")
        thi_set = sem("thi_set")
        tables_set = sem("tables_set")
        wst_set = sem("wst_set")
        sums_zero = sem("sums_zero")
        numb_in = [sem(f"numb_in{h}") for h in range(2)]
        fchunk_in = [sem(f"fchunk_in{h}") for h in range(2)]
        gsel_set = sem("gsel_set")
        numc_set = sem("numc_set")
        gath6_done = sem("gath6_done")
        gath7_done = sem("gath7_done")
        gath6_free = sem("gath6_free")
        x6_set = sem("x6_set")
        x_set = sem("x_set")
        msg_set = sem("msg_set")
        mhi_set = sem("mhi_set")
        mlo_set = sem("mlo_set")
        sum_done = sem("sum_done")
        sums_out = sem("sums_out")
        z_ps = sem("z_ps")
        z_set = sem("z_set")
        zl_set = sem("zl_set")
        o_ps = sem("o_ps")
        o_set = sem("o_set")
        h_set = sem("h_set")
        y_ps = sem("y_ps")
        y_seq = sem("y_seq")
        var_set = sem("var_set")
        std_set = sem("std_set")
        y_set = sem("y_set")
        s_out = sem("s_out")
        pool_go = sem("pool_go")
        pe_go = sem("pe_go")

        AB_STEPS = -(-NB // 2)
        T_PARTS = 5
        T_BLOCKS = NB // T_PARTS
        WIDE = [(n, min(BANK, NODES - n * BANK)) for n in range(BANKS)]
        YSTEPS = -(-NB // 4)
        W_DMAS = 8
        PADDED_MAP = STEP * LAG
        S0 = TURNS * STEPS

        LO_AHEAD = 3
        LOC_STEP = 12

        block = ctx.enter_context(nc.Block())

        @block.sync
        def _(sp):
            sp.dma_start(iota[:, :], c_iota).then_inc(s_const, 16)
            sp.dma_start(part[:, :], c_part).then_inc(s_const, 16)
            sp.dma_start(src_t[:, :], src.rearrange("(p j) -> p j", p=P)).then_inc(s_edges, 16)
            sp.dma_start(dst_t[:, :], dst.rearrange("(p j) -> p j", p=P)).then_inc(s_edges, 16)
            sp.dma_start(tri[:, :, :], c_tri).then_inc(s_const, 16)
            sp.dma_start(ident[:, :], c_ident).then_inc(s_const, 16)
            sp.dma_start(tiles_c[:, :], c_tiles).then_inc(s_const, 16)
            sp.dma_start(steps_c[:, :, :], c_steps).then_inc(s_const, 16)
            sp.dma_start(ef_t, ef.rearrange("(p j) f -> p (j f)", p=P)).then_inc(s_ef, 16)
            sp.dma_start(x0, x.rearrange("(b p) f -> p b f", p=P)).then_inc(s_x, 16)
            sp.wait_ge(blank_set, 2)
            for c0, c1 in ((2, CHUNKS // 2), (CHUNKS // 2, CHUNKS)):
                sp.dma_start(records[c0 * CHUNK * P:c1 * CHUNK * P, :].rearrange("(c p t) f -> p c (t f)", p=P, t=CHUNK),
                             blank[:, :, :].rearrange("p t f -> p (t f)").unsqueeze(1)
                             .to_broadcast([P, c1 - c0, CHUNK * RW])).then_inc(blanked, 16)
            for h in range(PREP):
                sp.dma_start(feat_d[h * EF:(h + 1) * EF, TILES * P:TILES * P + RW], blank[0:EF, 0, :].bitcast(F16)[:, 0:RW])\
                  .then_inc(feat_out[h], 16)
                sp.dma_start(nums_d[TILES * 2 + h * CHUNK:TILES * 2 + (h + 1) * CHUNK, 0:RW],
                             blank[0:CHUNK, 0, :].bitcast(F16)[:, 0:RW]).then_inc(nums_out[h], 16)
            sp.wait_ge(map_ready, 1)
            sp.dma_start(map_d[:, :].rearrange("(q p) s -> p q s", p=P), map_i[:, :, :]).then_inc(map_out, 16)
            sp.wait_ge(map_out, 16)
            sp.dma_start(map_row[:, :], map_d[:, :].rearrange("(a q) s -> a (q s)", a=1)).then_inc(map_in, 16)
            with sp.Fori(0, CHUNKS // PREP) as it:
                for h in range(PREP):
                    sp.wait_ge(featT_set, it * PREP + h + 1 + AHEAD)
                    sp.dma_start(feat_d[:, ds((it * PREP + h) * (CHUNK * P), CHUNK * P)], featT[:, h, :])\
                      .then_inc(feat_out[h], 16)
                    sp.wait_ge(numT_set, it * PREP + h + 1 + AHEAD)
                    sp.dma_start(nums_d[ds((it * PREP + h) * (2 * CHUNK), 2 * CHUNK), :], numT[:, h, :])\
                      .then_inc(nums_out[h], 16)
            for h in range(PREP):
                sp.wait_ge(feat_out[h], 16 * (CHUNKS // PREP + 1))
                sp.wait_ge(nums_out[h], 16 * (CHUNKS // PREP + 1))
            sp.dma_start(feat_d[:, TILES * P:(TILES + HALF) * P], feat_d[:, 0:HALF * P]).then_inc(wrap_out, 16)
            sp.dma_start(nums_d[TILES * 2:(TILES + HALF) * 2, :], nums_d[0:HALF * 2, :]).then_inc(wrap_out, 16)
            sp.wait_ge(wrap_out, 32)

            def load_half(c, h):
                sp.dma_start(numb[:, h, :], nums_d[ds(c * (2 * HALF), 2 * HALF), :].rearrange("(a k) e -> a (k e)", a=1)
                             .to_broadcast([P, HALF * 2 * P])).then_inc(numb_in[h], 16)
                sp.dma_start(fchunk[:, h, :], feat_d[:, ds(c * (HALF * P), HALF * P)]).then_inc(fchunk_in[h], 16)

            load_half(0, 0)
            with sp.Fori(0, L) as l:
                sp.wait_ge(o_ps, l * BANKS + AHEAD)
                sp.dma_start(wab[:, :, :], We1[ds(l, 1), 0:2 * D, :].rearrange("a (s k) f -> k (a s) f", s=2))\
                  .then_inc(w_in, 16)
                for r in range(4):
                    sp.dma_start(wc[r * EF:(r + 1) * EF, :],
                                 We1[ds(l, 1), 2 * D:2 * D + EF, :].rearrange("a k f -> (a k) f")).then_inc(w_in, 16)
                sp.dma_start(we2[:, :], We2[ds(l, 1), :, :].rearrange("a k f -> (a k) f")).then_inc(w_in, 16)
                sp.dma_start(wn1[:, :, :], Wn1[ds(l, 1), :, :].rearrange("a (s k) f -> k (a s) f", s=2))\
                  .then_inc(w_in, 16)
                sp.dma_start(wn2[:, :], Wn2[ds(l, 1), :, :].rearrange("a k f -> (a k) f")).then_inc(w_in, 16)
                with sp.Fori(0, TURNS) as it:
                    for h in range(2):
                        half = it * 2 + h
                        sp.wait_ge(gsel_set, l * (2 * TURNS) + half + 1)
                        sp.wait_ge(gath7_done, l * S0 + half * (STEPS // 2) + AHEAD)
                        load_half(half + 1, 1 - h)
            sp.wait_ge(sum_done, L * S0 + AHEAD)
            sp.dma_start(xn, x.rearrange("(b p) f -> p b f", p=P)).then_inc(s_x, 16)
            sp.wait_ge(y_set, 1)
            full = N // P
            sp.dma_start(out[0:full * P, :].rearrange("(b p) f -> p b f", p=P), y[:, 0:full, :]).then_inc(s_out, 16)
            sp.dma_start(out[full * P:N, :], y[0:N - full * P, full, :]).then_inc(s_out, 16)
            sp.wait_ge(s_out, 32)
            sp.wait_ge(numb_in[0], 16 * (1 + L * TURNS))
            sp.wait_ge(fchunk_in[0], 16 * (1 + L * TURNS))

        @block.gpsimd
        def _(pool):
            pool.memset(blank[:, :, 0:EF], 0.0).then_inc(blank_set, 1)
            pool.memset(blank[:, :, EF:RW], -1.0).then_inc(blank_set, 1)
            pool.wait_ge(blank_set, 2)
            for h in range(2):
                pool.dma_start(records[h * CHUNK * P:(h + 1) * CHUNK * P, :].rearrange("(p t) f -> p (t f)", t=CHUNK),
                               blank[:, :, :].rearrange("p t f -> p (t f)")).then_inc(moved[h], 16)
            pool.wait_ge(moved[0], 16)
            pool.wait_ge(moved[1], 16)
            pool.wait_ge(blanked, 32)
            with pool.Fori(0, GTURNS) as it:
                for h in range(2):
                    pool.wait_ge(rec_set, it * 2 + h + 1)
                    pool.wait_ge(rows_set, it * 2 + h + 1)
                    pool.sem_inc(pool_go, 1)
                    for g in range(GROUP):
                        pool.indirect_dma_start(
                            out=records[:, :],
                            out_offset=bass.IndirectOffsetOnAxis(ap=rowi[:, h, g:g + 1].bitcast(U32), axis=0),
                            in_=rec[:, h, g, :], in_offset=None).then_inc(moved[h], 16)
            pool.wait_ge(efmax_ready, 1)
            pool.partition_all_reduce(efmax[:, 1:2], efmax[:, 0:1], P, bass.bass_isa.ReduceOp.max).then_inc(efmax_all, 1)
            for h in range(2):
                pool.wait_ge(moved[h], 16 * GROUP * GTURNS + 16)
            with pool.Fori(0, CHUNKS // PREP) as it:
                for h in range(PREP):
                    pool.wait_ge(recc_used[h], it + AHEAD)
                    pool.dma_start(recc[:, h, :, :].rearrange("p t f -> p (t f)"),
                                   records[ds((it * PREP + h) * (CHUNK * P), CHUNK * P), :]
                                   .rearrange("(p t) f -> p (t f)", p=P)).then_inc(recc_in[h], 16)
            with pool.Fori(0, L) as l:
                pool.wait_ge(mx_set, l + 1)
                pool.sem_inc(pool_go, 1)
                pool.partition_all_reduce(mxa[:, :], mx[:, :], P, bass.bass_isa.ReduceOp.max).then_inc(mx_all, 1)
                with pool.Fori(0, TURNS) as it:
                    step0 = l * S0 + it * STEPS
                    for q in range(STEPS):
                        place = (q - 1) % RING
                        pool.wait_ge(mhi_set, step0 + q + 1)
                        pool.tensor_tensor(m_lo[:, place, :], msg[:, place, :], m_hi[:, place, :], ALU.subtract)\
                            .then_inc(mlo_set, 1)

        @block.scalar
        def _(act):
            for s in (featT_set, o_set, x_set):
                act.sem_inc(s, AHEAD)
            for n in range(BANKS):
                w = WIDE[n][1]
                act.wait_ge(hT_ps, n + 1)
                act.activation(hT[:, n * BANK:n * BANK + w], sums[:, n * BANK:n * BANK + w], ACT.Copy).then_inc(hT_in, 1)
            act.wait_ge(s_ef, 16)
            act.wait_ge(dve_seq, LOC_STEP)
            with act.Fori(0, GTURNS) as it:
                for h in range(2):
                    col = it * (2 * GROUP) + h * GROUP
                    act.wait_ge(moved[h], it * (16 * GROUP) + 16)
                    act.activation(rec[:, h, :, 0:EF], ef_t[:, ds(col * EF, GROUP * EF)]
                                   .rearrange("p (g f) -> p g f", f=EF), ACT.Copy)
                    act.activation(rec[:, h, :, EF:RW], loc[:, ds(col, GROUP), :], ACT.Copy).then_inc(rec_set, 1)
            act.wait_ge(scef_ready, 1)
            with act.Fori(0, CHUNKS // PREP) as it:
                act.wait_ge(tr_done, it * PREP + AHEAD)
                for h in range(PREP):
                    act.wait_ge(recc_in[h], it * 16 + 16)
                    act.activation(stack[:, h, :, 0, :], recc[:, h, :, 0:EF], ACT.Copy, scale=sc_ef[:, 0:1])\
                       .then_inc(fhi_set, 1)
                for h in range(PREP):
                    act.wait_ge(tr_done, it * PREP + h + 1 + AHEAD)
                    act.wait_ge(feat_out[h], it * 16 + 16)
                    act.activation(featT[:, h, :], bank(h)[0:4 * EF, :].bitcast(F16), ACT.Copy).then_inc(featT_set, 1)
            with act.Fori(0, L) as l:
                act.wait_ge(w2t_ps, l + 1)
                act.activation(we2T[:, :], gath[:, 0:D], ACT.Copy).then_inc(w2t_set, 1)
                act.wait_ge(w21_ps, l + 1)
                act.activation(w21[:, :], gath[:, 0:D], ACT.Copy).then_inc(w21_set, 1)
                for s in range(AB_STEPS):
                    n0, n1 = s * 2 * P, min((s + 1) * 2 * P, NODES)
                    act.wait_ge(ab_ps, l * AB_STEPS + s + 1)
                    act.activation(ab3[:, :, n0:n1], planes_of(bank(s % 6))[:, :, 0:n1 - n0], ACT.Copy).then_inc(ab_set, 1)
                act.wait_ge(sc_set, l + 1)
                for s in range(T_PARTS):
                    b0, b1 = s * T_BLOCKS, (s + 1) * T_BLOCKS
                    act.activation(two_planes(t_hi, b0, b1), ab3[:, :, b0 * P:b1 * P], ACT.Copy, scale=sc[:, 0:1])\
                       .then_inc(thi_set, 1)
                with act.Fori(0, TURNS) as it:
                    step0 = l * S0 + it * STEPS
                    for q in range(STEPS):
                        place = q % RING
                        act.wait_ge(gath6_done, step0 + q + 1)
                        act.wait_ge(mlo_set, step0 + q + LO_AHEAD - RING + 2)
                        act.activation(msg[:, place, 0:2 * D], gath6, ACT.Copy).then_inc(x6_set, 1)
                        act.wait_ge(x6_set, step0 + q + 1)
                        act.activation(gath6, iota[:, 0:2 * D], ACT.Copy, scale=0.0).then_inc(gath6_free, 1)
                        act.wait_ge(gath7_done, step0 + q + 1 + AHEAD)
                        act.activation(msg[:, place, 2 * D:MSG], gath[:, :], ACT.Copy).then_inc(x_set, 1)
                        act.wait_ge(msg_set, step0 + q + AHEAD)
                        act.wait_ge(sum_done, step0 + q + AHEAD)
                        act.activation(m_hi[:, (q - 1) % RING, :], msg[:, (q - 1) % RING, :], ACT.Copy)\
                           .then_inc(mhi_set, 1)
                act.wait_ge(sum_done, (l + 1) * S0 + AHEAD)
                for n in range(BANKS):
                    w = WIDE[n][1]
                    act.activation(sumS[:, n * BANK:n * BANK + w], sums[:, n * BANK:n * BANK + w], ACT.Copy,
                                   scale=sc[:, 1:2]).then_inc(sums_out, 1)
                for n in range(BANKS):
                    w = WIDE[n][1]
                    act.wait_ge(z_ps, l * BANKS + n + 1)
                    act.activation(zbuf[:, n * BANK:n * BANK + w], sums[:, n * BANK:n * BANK + w], ACT.Copy)\
                       .then_inc(z_set, 1)
                for n in range(BANKS):
                    w = WIDE[n][1]
                    act.wait_ge(o_ps, l * BANKS + n + 1 + AHEAD)
                    act.wait_ge(h_set, l * BANKS + n + 1 + AHEAD)
                    act.activation(outT[:, n * BANK:n * BANK + w], sums[:, n * BANK:n * BANK + w], ACT.Copy)\
                       .then_inc(o_set, 1)
            act.wait_ge(var_set, 1)
            act.activation(rstd[:, :], rstd[:, :], ACT.Sqrt).then_inc(std_set, 1)

        @block.vector
        def _(dve):
            steps = [0]

            def then(ins):
                steps[0] += 1
                ins.then_inc(dve_seq, 1)
                dve.wait_ge(dve_seq, steps[0])

            def exponent(dst, field, shift_bits, sign):
                return dve.tensor_scalar(dst.bitcast(I32), field, float(sign), float(shift_bits * EXP1), ALU.mult, ALU.add)

            for s in (msg_set, hot_set, numT_set, h_set, *recc_used):
                dve.sem_inc(s, AHEAD)
            dve.sem_inc(mlo_set, LO_AHEAD)
            dve.wait_ge(s_const, 16 * 6)
            dve.wait_ge(s_edges, 32)
            then(dve.tensor_tensor(lo_n[:, :], src_t[:, :], dst_t[:, :], ALU.min))
            then(dve.tensor_tensor(hi_n[:, :], src_t[:, :], dst_t[:, :], ALU.max))
            then(dve.tensor_scalar(lo_b, lo_n[:, :], 7, None, ALU.logical_shift_right))
            then(dve.tensor_scalar(hi_b, hi_n[:, :], 7, None, ALU.logical_shift_right))
            then(dve.tensor_scalar(src_t[:, :], lo_n[:, :], P - 1, None, ALU.bitwise_and))
            then(dve.tensor_scalar(dst_t[:, :], hi_n[:, :], P - 1, None, ALU.bitwise_and))
            then(dve.tensor_scalar(key[:, :], hi_b, float(NB), float(-DEAD), ALU.is_equal, ALU.mult))
            then(dve.tensor_tensor(loc[:, :, 0], src_t[:, :], key[:, :], ALU.add))
            then(dve.tensor_tensor(loc[:, :, 1], dst_t[:, :], key[:, :], ALU.add))
            then(dve.tensor_copy(ident16[:, :], ident[:, :]))
            then(dve.memset(zeros[:, :], 0.0))
            then(dve.memset(zeros16[:, :], 0.0))
            assert steps[0] == LOC_STEP
            then(dve.scalar_tensor_tensor(key[:, :], hi_b, 1.0, hi_b, ALU.add, ALU.mult))
            then(dve.scalar_tensor_tensor(key[:, :], key[:, :], 0.5, lo_b, ALU.mult, ALU.add))

            def keys(it, after):
                dve.wait_ge(hot_set, it * (2 * GROUP) + after * (2 * GROUP) + AHEAD)
                dve.tensor_copy(keyc[:, :], key[:, ds(it * (2 * GROUP), 2 * GROUP)]).then_inc(keyc_set, 1)
                dve.wait_ge(keyc_set, after + it + 1)

            def one_hot(k):
                dve.tensor_scalar(onehot[:, k, :], iota[:, 0:BUCKETS], keyc[:, k:k + 1], None, ALU.is_equal)\
                   .then_inc(hot_set, 1)

            with dve.Fori(0, GTURNS) as it:
                keys(it, 0)
                dve.wait_ge(hist_half, it * 2 + AHEAD)
                for h in range(2):
                    for g in range(GROUP):
                        one_hot(h * GROUP + g)
            dve.wait_ge(hist_half, 2 * GTURNS + AHEAD)
            then(dve.tensor_copy(cnt_i[:, :], bank(0)[:, 0:BUCKETS]))
            then(dve.tensor_scalar(cnt_i[:, :], cnt_i[:, :], float(P - 1), None, ALU.add))
            then(dve.tensor_scalar(cnt_i[:, :], cnt_i[:, :], 7, None, ALU.logical_shift_right))
            then(dve.tensor_copy(cnt_f[:, :], cnt_i[:, :]))
            then(dve.tensor_tensor_scan(tile_end[:, :], cnt_f[:, :], zeros[:, :], 0.0, ALU.add, ALU.add))
            dve.tensor_tensor(tile_beg[:, :], tile_end[:, :], cnt_f[:, :], ALU.subtract).then_inc(beg_ready, 1)
            for q in range(MAPQ):
                for s in range(2):
                    then(dve.scalar_tensor_tensor(scrap[:, :], tile_end[:, :], tiles_c[:, q:q + 1], steps_c[:, s, :],
                                                  ALU.is_le, ALU.mult, accum_out=map_f[:, q, s:s + 1]))
            dve.tensor_copy(map_i[:, :, :], map_f[:, :, :]).then_inc(map_ready, 1)
            with dve.Fori(0, GTURNS) as it:
                keys(it, GTURNS)
                for h in range(2):
                    one_hot(h * GROUP)
                    for g in range(GROUP):
                        if g + 1 < GROUP:
                            one_hot(h * GROUP + g + 1)
                        dve.wait_ge(rank_set, it * (2 * GROUP) + (h * GROUP + g + 1))
                        dve.scalar_tensor_tensor(scrap[:, :], bank(1)[:, 0:BUCKETS], 1.0, onehot[:, h * GROUP + g, :],
                                                 ALU.mult, ALU.mult, accum_out=slot_f[:, g:g + 1]).then_inc(rank_read, 1)
                    row0 = it * 10 + h * 5
                    dve.wait_ge(rank_read, it * (2 * GROUP) + (h + 1) * GROUP)
                    dve.tensor_copy(slot_i[:, :], slot_f[:, :]).then_inc(rows_seq, 1)
                    dve.wait_ge(rows_seq, row0 + 1)
                    dve.tensor_scalar(rowa[:, :], slot_i[:, :], P - 1, 3, ALU.bitwise_and, ALU.logical_shift_left)\
                       .then_inc(rows_seq, 1)
                    dve.wait_ge(rows_seq, row0 + 2)
                    dve.tensor_scalar(rowb[:, :], slot_i[:, :], 7, CHUNK - 1, ALU.logical_shift_right, ALU.bitwise_and)\
                       .then_inc(rows_seq, 1)
                    dve.wait_ge(rows_seq, row0 + 3)
                    dve.tensor_tensor(rowa[:, :], rowa[:, :], rowb[:, :], ALU.bitwise_or).then_inc(rows_seq, 1)
                    dve.wait_ge(rows_seq, row0 + 4)
                    dve.tensor_scalar(slot_i[:, :], slot_i[:, :], 10, 10, ALU.logical_shift_right, ALU.logical_shift_left)\
                       .then_inc(rows_seq, 1)
                    dve.wait_ge(rows_seq, row0 + 5)
                    dve.wait_ge(moved[h], it * (16 * GROUP) + 16)
                    dve.tensor_tensor(rowi[:, h, :], rowa[:, :], slot_i[:, :], ALU.bitwise_or).then_inc(rows_set, 1)
            dve.wait_ge(s_ef, 16)
            dve.tensor_reduce(efmax[:, 0:1], ef_t, AX_X, ALU.max, apply_absolute_value=True).then_inc(efmax_ready, 1)
            dve.wait_ge(efmax_all, 1)
            then(dve.tensor_scalar(bnd[:, 0:1], efmax[:, 1:2], 2.0 ** -100, None, ALU.max))
            then(dve.tensor_scalar(ebits[:, 0:1], bnd[:, 0:1].bitcast(I32), EXP_MASK, None, ALU.bitwise_and))
            then(exponent(sc_ef[:, 0:1], ebits[:, 0:1], 259, -1))
            exponent(sc_ef[:, 1:2], ebits[:, 0:1], -5, 1).then_inc(scef_ready, 1)
            dve.wait_ge(scef_ready, 1)
            with dve.Fori(0, CHUNKS // PREP) as it:
                for h in range(PREP):
                    c = it * PREP + h
                    dve.wait_ge(recc_in[h], it * 16 + 16)
                    dve.tensor_copy(numcol[:, ds(c * (2 * CHUNK), 2 * CHUNK)].rearrange("p (t s) -> p t s", s=2),
                                    recc[:, h, :, EF:RW])
                    dve.wait_ge(tr_done, it * PREP + AHEAD)
                    dve.tensor_copy(num16[:, h, :].rearrange("p (t s) -> p t s", s=2), recc[:, h, :, EF:RW])
                    dve.wait_ge(fhi_set, c + 1)
                    dve.scalar_tensor_tensor(stack[:, h, :, 1, :], recc[:, h, :, 0:EF], sc_ef[:, 0:1],
                                             stack[:, h, :, 0, :], ALU.mult, ALU.subtract).then_inc(recc_used[h], 1)
                    dve.wait_ge(recc_used[h], it + 1 + AHEAD)
                    dve.tensor_copy(stack[:, h, :, 2:4, :], stack[:, h, :, 0:2, :]).then_inc(fst_set, 1)
                for h in range(PREP):
                    dve.wait_ge(tr_done, it * PREP + h + 1 + AHEAD)
                    dve.wait_ge(nums_out[h], it * 16 + 16)
                    dve.tensor_copy(numT[:, h, :], bank(PREP + h)[0:2 * CHUNK, 0:P // 2].bitcast(F16)).then_inc(numT_set, 1)
            then(dve.memset(ssel[:, ITER - STEP * LAG:ITER, :, :], 0.0))
            then(dve.memset(mx[:, :], 0.0))
            dve.memset(msg[:, RING - 1, :], 0.0)
            dve.memset(m_hi[:, RING - LAG:RING, :], 0.0)
            then(dve.memset(m_lo[:, RING - LAG:RING, :], 0.0))

            def leaky(m):
                return dve.scalar_tensor_tensor(m, m, SLOPE, m, ALU.mult, ALU.max)

            def gather_one_hot(h):
                dve.tensor_scalar(gsel[:, h, :], numb[:, h, :], part[:, 0:1], None, ALU.is_equal).then_inc(gsel_set, 1)

            dve.wait_ge(numb_in[0], 16)
            gather_one_hot(0)
            with dve.Fori(0, L) as l:
                dve.wait_ge(w_in, (l + 1) * (16 * W_DMAS))
                dve.tensor_reduce(mx[0:4 * EF, 1:2], wc[:, :], AX_X, ALU.max, apply_absolute_value=True)
                for s in range(AB_STEPS):
                    n0, n1 = s * 2 * P, min((s + 1) * 2 * P, NODES)
                    dve.wait_ge(ab_set, l * AB_STEPS + s + 1)
                    dve.tensor_reduce(abmax[:, s, :], ab3[:, :, n0:n1], AX_X, ALU.max,
                                      apply_absolute_value=True).then_inc(ab_maxed, 1)
                dve.wait_ge(ab_maxed, (l + 1) * AB_STEPS)
                dve.tensor_reduce(mx[:, 0:1], abmax[:, 0:AB_STEPS, :].rearrange("p s k -> p (s k)"), AX_X, ALU.max).then_inc(mx_set, 1)
                dve.memset(sums[:, :], 0.0).then_inc(sums_zero, 1)
                dve.wait_ge(mx_all, l + 1)
                seq = l * 6
                dve.tensor_tensor(bnd[:, 0:1], mxa[:, 1:2], efmax[:, 1:2], ALU.mult)\
                   .then_inc(sc_seq, 1)
                dve.tensor_scalar(bnd[:, 1:2], mxa[:, 0:1], 2.0, 2.0 ** -100, ALU.mult, ALU.max).then_inc(sc_seq, 1)
                dve.wait_ge(sc_seq, seq + 2)
                dve.scalar_tensor_tensor(bnd[:, 0:1], bnd[:, 0:1], float(EF), bnd[:, 1:2], ALU.mult, ALU.add)\
                   .then_inc(sc_seq, 1)
                dve.wait_ge(sc_seq, seq + 3)
                dve.tensor_scalar(ebits[:, 0:1], bnd[:, 0:1].bitcast(I32), EXP_MASK, None, ALU.bitwise_and)\
                   .then_inc(sc_seq, 1)
                dve.wait_ge(sc_seq, seq + 4)
                exponent(sc[:, 0:1], ebits[:, 0:1], 268, -1).then_inc(sc_seq, 1)
                dve.wait_ge(sc_seq, seq + 5)
                exponent(sc[:, 1:2], ebits[:, 0:1], -14, 1).then_inc(sc_set, 1)
                dve.tensor_scalar(sc_w[:, :], sc[:, 0:1], sc_ef[:, 1:2], 2.0 ** 120, ALU.mult, ALU.min).then_inc(sc_seq, 1)
                dve.wait_ge(sc_seq, seq + 6)
                wseq = l * 4
                dve.tensor_scalar(wcs[:, :], wc[:, :], sc_w[0:4 * EF, 0:1], None, ALU.mult).then_inc(wst_set, 1)
                dve.wait_ge(wst_set, wseq + 1)
                dve.tensor_copy(wch[:, :], wcs[:, :]).then_inc(wst_set, 1)
                dve.wait_ge(wst_set, wseq + 2)
                for k in range(2):
                    dve.tensor_copy(wst[0:2 * EF, k, :], wch[0:2 * EF, :])
                    last = dve.tensor_tensor(wst[2 * EF:4 * EF, k, :], wcs[2 * EF:4 * EF, :], wch[2 * EF:4 * EF, :],
                                             ALU.subtract)
                    last.then_inc(wst_set, 1)
                for s in range(T_PARTS):
                    b0, b1 = s * T_BLOCKS, (s + 1) * T_BLOCKS
                    dve.wait_ge(thi_set, l * T_PARTS + s + 1)
                    dve.tensor_copy(t_hi[:, 2 * NODES + b0 * P:2 * NODES + b1 * P], t_hi[:, b0 * P:b1 * P])
                    dve.scalar_tensor_tensor(two_planes(t_lo, b0, b1), ab3[:, :, b0 * P:b1 * P], sc[:, 0:1],
                                             two_planes(t_hi, b0, b1), ALU.mult, ALU.subtract).then_inc(tables_set, 1)
                dve.wait_ge(tables_set, l * (T_PARTS + 1) + T_PARTS)
                dve.tensor_copy(t_lo[:, 2 * NODES:3 * NODES], t_lo[:, 0:NODES]).then_inc(tables_set, 1)
                with dve.Fori(0, TURNS) as it:
                    step0 = l * S0 + it * STEPS
                    turn = l * TURNS + it
                    dve.wait_ge(msg_set, step0 + AHEAD)
                    dve.tensor_copy(numc[:, :], numcol[:, ds(it * (2 * ITER), 2 * ITER)]).then_inc(numc_set, 1)
                    dve.wait_ge(numc_set, turn + 1)
                    for q in range(STEPS):
                        for t in range(STEP * q, STEP * q + STEP):
                            for s in range(2):
                                dve.tensor_scalar(ssel[:, t, s, :], iota[:, 0:P], numc[:, 2 * t + s:2 * t + s + 1], None,
                                                  ALU.is_equal)
                        dve.wait_ge(x_set, step0 + q + 1 + AHEAD)
                        leaky(msg[:, q % RING, :]).then_inc(msg_set, 1)
                        if q % (STEPS // 2) == 1:
                            h = q // (STEPS // 2)
                            half = it * 2 + h
                            dve.wait_ge(gath7_done, l * S0 + half * (STEPS // 2) + AHEAD)
                            dve.wait_ge(numb_in[1 - h], turn * 16 + (32 if h else 16))
                            gather_one_hot(1 - h)
                for n in range(BANKS):
                    w = WIDE[n][1]
                    dve.wait_ge(z_set, l * BANKS + n + 1)
                    leaky(zbuf[:, n * BANK:n * BANK + w]).then_inc(zl_set, 1)
                for n in range(BANKS):
                    w = WIDE[n][1]
                    part_n = slice(n * BANK, n * BANK + w)
                    dve.wait_ge(o_ps, l * BANKS + n + 1 + AHEAD)
                    dve.tensor_tensor(hT[:, part_n], hT[:, part_n], sums[:, part_n], ALU.add).then_inc(h_set, 1)
            for n in range(YSTEPS):
                b0, b1 = 4 * n, min(4 * n + 4, NB)
                w = (b1 - b0) * D
                dve.wait_ge(y_ps, n + 1)
                dve.wait_ge(s_x, 32)
                dve.tensor_tensor(y[:, b0:b1, :].rearrange("p b f -> p (b f)"), sums[:, n * BANK:n * BANK + w],
                                  xn[:, b0:b1, :].rearrange("p b f -> p (b f)"), ALU.add).then_inc(y_seq, 1)
            dve.wait_ge(y_seq, YSTEPS)
            for b in range(NB):
                dve.bn_stats(stats[:, b, :], y[:, b, :]).then_inc(y_seq, 1)
            dve.wait_ge(y_seq, YSTEPS + NB)
            for b in range(NB):
                dve.bn_aggr(mv[:, b, :], stats[:, b, :]).then_inc(y_seq, 1)
            dve.wait_ge(y_seq, YSTEPS + 2 * NB)
            dve.tensor_scalar(rstd[:, :], mv[:, :, 1], 1e-5, None, ALU.add).then_inc(var_set, 1)
            dve.wait_ge(std_set, 1)
            dve.reciprocal(rstd[:, :], rstd[:, :]).then_inc(y_seq, 1)
            dve.wait_ge(y_seq, YSTEPS + 2 * NB + 1)
            for b in range(NB):
                last = dve.tensor_scalar(y[:, b, :], y[:, b, :], mv[:, b, 0:1], rstd[:, b:b + 1], ALU.subtract, ALU.mult)
            last.then_inc(y_set, 1)

        @block.tensor
        def _(pe):
            for s in (gath7_done, tr_done, sum_done, hist_half, o_ps):
                pe.sem_inc(s, AHEAD)
            pe.wait_ge(s_const, 16 * 6)
            pe.wait_ge(s_x, 16)
            for b in range(NB):
                last = pe.transpose(sums[:, b * P:(b + 1) * P], x0[:, b, :], ident[:, :])
                if b % 4 == 3 or b == NB - 1:
                    last.then_inc(hT_ps, 1)
            pe.wait_ge(hT_in, BANKS)
            hist = bank(0)[:, 0:BUCKETS]
            pe.wait_ge(dve_seq, LOC_STEP)
            pe.matmul(hist, tri[:, 2, :], zeros16[:, :], start=True, stop=False, skip_group_check=True)
            with pe.Fori(0, GTURNS) as it:
                for h in range(2):
                    for g in range(GROUP):
                        pe.wait_ge(hot_set, it * (2 * GROUP) + (h * GROUP + g + 1) + AHEAD)
                        last = pe.matmul(hist, tri[:, 2, :], onehot[:, h * GROUP + g, :], start=False, stop=False,
                                         skip_group_check=True)
                    last.then_inc(hist_half, 1)
            pe.wait_ge(beg_ready, 1)
            rank = bank(1)[:, 0:BUCKETS]
            pe.matmul(rank, tri[:, 2, :], tile_beg[:, :], start=True, stop=False, skip_group_check=True)
            with pe.Fori(0, GTURNS) as it:
                for k in range(2 * GROUP):
                    pe.wait_ge(hot_set, it * (2 * GROUP) + (COLS + k + 1) + AHEAD)
                    pe.matmul(rank, tri[:, 0, :], onehot[:, k, :], start=False, stop=False, skip_group_check=True)\
                      .then_inc(rank_set, 1)
                    pe.wait_ge(rank_read, it * (2 * GROUP) + (k + 1))
                    pe.matmul(rank, tri[:, 1, :], onehot[:, k, :], start=False, stop=False, skip_group_check=True)
            with pe.Fori(0, CHUNKS // PREP) as it:
                for h in range(PREP):
                    pe.wait_ge(dve_seq, LOC_STEP)
                    pe.wait_ge(fst_set, it * PREP + h + 1)
                    pe.wait_ge(featT_set, it * PREP + AHEAD)
                    pe.wait_ge(numT_set, it * PREP + AHEAD)
                    pe.sem_inc(pe_go, 1)
                    for t in range(CHUNK):
                        pe.transpose(bank(h)[0:4 * EF, t * P // 2:(t + 1) * P // 2].bitcast(F16),
                                     stack[:, h, t, :, :].rearrange("p k f -> p (k f)"), ident16[:, :])
                    pe.transpose(bank(PREP + h)[0:2 * CHUNK, 0:P // 2].bitcast(F16), num16[:, h, :], ident16[:, :])\
                      .then_inc(tr_done, 1)
            with pe.Fori(0, L) as l:
                pe.wait_ge(w_in, (l + 1) * (16 * W_DMAS))
                pe.transpose(gath[:, 0:D], we2[:, :], ident[:, :]).then_inc(w2t_ps, 1)
                pe.wait_ge(w2t_set, l + 1)
                pe.matmul(gath[:, 0:D], we2T[:, :], wn1[:, 1, :], start=True, stop=True).then_inc(w21_ps, 1)
                pe.wait_ge(h_set, l * BANKS + AHEAD)
                pe.wait_ge(o_set, l * BANKS + AHEAD)
                for s in range(AB_STEPS):
                    if s >= 6:
                        pe.wait_ge(ab_set, l * AB_STEPS + s - 5)
                    for b in range(2 * s, min(2 * s + 2, NB)):
                        last = pe.matmul(planes_of(bank(s % 6))[:, :, (b % 2) * D:(b % 2 + 1) * D], hT[:, b * P:(b + 1) * P],
                                         wab[:, :, :], start=True, stop=True)
                    last.then_inc(ab_ps, 1)
                pe.wait_ge(w21_set, l + 1)
                pe.wait_ge(tables_set, (l + 1) * (T_PARTS + 1))
                pe.wait_ge(map_in, 16)
                pe.wait_ge(wst_set, (l + 1) * 4)
                pe.wait_ge(sums_zero, l + 1)
                pe.sem_inc(pe_go, 1)
                with pe.Fori(0, TURNS) as it:
                    step0 = l * S0 + it * STEPS
                    turn = l * TURNS + it

                    def blocks(first, n):
                        _, v = nc.values_load_multi_w_load_instructions(
                            map_row[0:1, ds(it * (2 * ITER) + 2 * (first + PADDED_MAP), 2 * n)],
                            engines=(mybir.EngineType.PE,), min_val=0, max_val=(NB - 1) * P,
                            skip_runtime_bounds_check_because="sums of the constant steps over the first buckets")
                        return {first + t: (v[2 * t], v[2 * t + 1]) for t in range(n)}

                    def rows(t, node0, plane):
                        return t[:, plane * NODES:(plane + 2) * NODES].rearrange("p (k n) -> p k n", k=2)[:, :, ds(node0, P)]

                    def gather_rows(t):
                        lo, hi = of_tile[t]
                        return rows(t_hi, lo, 0), rows(t_lo, lo, 0), rows(t_hi, hi, 1), rows(t_lo, hi, 1)

                    def sum_places(t):
                        lo, hi = of_tile[t]
                        return sums[:, ds(lo, P)], sums[:, ds(hi, P)]

                    def addresses(t):
                        for ap in (*gather_rows(t), *sum_places(t - STEP * LAG)):
                            pe.lower_ap(ap)

                    def gather(uv, t, h, fresh):
                        tc = t % HALF
                        at = [gsel[:, h, (2 * tc + s) * P:(2 * tc + s + 1) * P] for s in range(2)]
                        pe.matmul(uv, fchunk[:, h, tc * P:(tc + 1) * P], wst[:, :, :].rearrange("p s f -> p (s f)"),
                                  start=fresh, stop=False, skip_group_check=True)
                        for n, r in enumerate(gather_rows(t)):
                            last = pe.matmul(uv, at[n // 2], r, start=False, stop=n == 3, skip_group_check=True)
                        return last

                    for q in range(STEPS):
                        h = q // (STEPS // 2)
                        if q % 2 == 0:
                            of_tile = blocks(STEP * (q - LAG), STEP * (LAG + 2))
                        t = STEP * q
                        addresses(t)
                        if q % (STEPS // 2) == 0:
                            pe.wait_ge(gsel_set, turn * 2 + h + 1)
                            pe.wait_ge(fchunk_in[h], turn * 16 + 16)
                            pe.sem_inc(pe_go, 1)
                        gather(gath6, t, h, False).then_inc(gath6_done, 1)
                        addresses(t + 1)
                        pe.wait_ge(x_set, step0 + q + AHEAD)
                        gather(gath[:, 0:2 * D], t + 1, h, True)
                        addresses(t + 2)
                        gather(gath[:, 2 * D:4 * D], t + 2, h, True).then_inc(gath7_done, 1)
                        pe.wait_ge(gath6_free, step0 + q + 1)
                        pe.wait_ge(mlo_set, step0 + q + LO_AHEAD - LAG + 2)
                        place = (q - LAG) % RING
                        for i in range(STEP):
                            at_lo, at_hi = sum_places(t + i - STEP * LAG)
                            ts = (t + i - STEP * LAG) % ITER
                            for s, out_n in ((1, at_hi), (0, at_lo)):
                                w0 = i * 2 * D + (1 - s) * D
                                for m in (m_hi, m_lo):
                                    last = pe.matmul(out_n, m[:, place, w0:w0 + D], ssel[:, ts, s, :], start=False,
                                                     stop=False, skip_group_check=True)
                        last.then_inc(sum_done, 1)
                for n in range(BANKS):
                    w = WIDE[n][1]
                    cols = slice(n * BANK, n * BANK + w)
                    pe.wait_ge(sums_out, l * BANKS + n + 1)
                    pe.matmul(sums[:, cols], wn1[:, 0, :], hT[:, cols], start=True, stop=False)
                    pe.matmul(sums[:, cols], w21[:, :], sumS[:, cols], start=False, stop=True).then_inc(z_ps, 1)
                for n in range(BANKS):
                    w = WIDE[n][1]
                    cols = slice(n * BANK, n * BANK + w)
                    pe.wait_ge(zl_set, l * BANKS + n + 1)
                    pe.matmul(sums[:, cols], wn2[:, :], zbuf[:, cols], start=True, stop=True).then_inc(o_ps, 1)
            for n in range(YSTEPS):
                b0, b1 = 4 * n, min(4 * n + 4, NB)
                pe.wait_ge(o_set, L * BANKS + AHEAD)
                for b in range(b0, b1):
                    last = pe.transpose(sums[:, b * P:(b + 1) * P], outT[:, b * P:(b + 1) * P], ident[:, :])
                last.then_inc(y_ps, 1)


def constants(np):
    i = np.arange(P)
    earlier = (i[:, None] < i[None, :]).astype(np.float16)
    tri = np.stack([earlier, 1 - earlier, np.ones_like(earlier)], axis=1)
    lo = [b for a in range(NB) for b in range(a + 1)] + [0, 0]
    hi = [a for a in range(NB) for b in range(a + 1)] + [0, 0]
    steps = P * np.stack([np.diff(lo), np.diff(hi)]).astype(np.float32)
    tiles = (np.arange(MAPQ)[None, :] * P + i[:, None] - STEP * LAG).astype(np.float32)
    return {
        "c_iota": np.ascontiguousarray(np.broadcast_to(np.arange(384, dtype=np.float16), (P, 384))),
        "c_part": i.astype(np.float32).reshape(P, 1),
        "c_tri": np.ascontiguousarray(tri),
        "c_ident": np.eye(P, dtype=np.float32),
        "c_tiles": np.ascontiguousarray(tiles),
        "c_steps": np.ascontiguousarray(np.broadcast_to(steps, (P, 2, BUCKETS))),
    }


def kernel(x, src, dst, edge_attr_16, L0_gnn_We1, L0_gnn_We2, L0_gnn_Wn1, L0_gnn_Wn2):
    import numpy as np
    import concourse.bacc as bacc
    from concourse.bass_utils import run_bass_kernel_spmd

    def padded(a, rows, fill):
        a = np.asarray(a)
        whole = np.full((rows,) + a.shape[1:], fill, a.dtype)
        whole[:a.shape[0]] = a
        return whole

    arrays = {
        "x": padded(x, NODES, 0),
        "src": padded(src, P * COLS, 0),
        "dst": padded(dst, P * COLS, NODES),
        "ef": padded(edge_attr_16, P * COLS, 0),
        "We1": np.ascontiguousarray(L0_gnn_We1),
        "We2": np.ascontiguousarray(L0_gnn_We2),
        "Wn1": np.ascontiguousarray(L0_gnn_Wn1),
        "Wn2": np.ascontiguousarray(L0_gnn_Wn2),
        **constants(np),
    }
    nc = bacc.Bacc("TRN2", target_bir_lowering=False, num_devices=1)
    args = {k: nc.dram_tensor(k, a.shape, mybir.dt.from_np(a.dtype), kind="ExternalInput").ap() for k, a in arrays.items()}
    out = nc.dram_tensor("out", (N, D), F32, kind="ExternalOutput").ap()
    build(nc, **args, out=out)
    r = run_bass_kernel_spmd(nc, [arrays], core_ids=[0])
    return r.results[0]["out"]
```
